# Optimizing a Trainium2 kernel written in Bass

```python
import numpy as np
import jax
import jax.numpy as jnp

def _softmax(x, axis=-1):
    return jax.nn.softmax(x, axis=axis)

def _gelu(x):
    return jax.nn.gelu(x, approximate=True)

def _silu(x):
    return jax.nn.silu(x)

def _sigmoid(x):
    return jax.nn.sigmoid(x)

def _layernorm(x, axis=-1, eps=1e-05):
    m = jnp.mean(x, axis=axis, keepdims=True)
    v = jnp.var(x, axis=axis, keepdims=True)
    return (x - m) / jnp.sqrt(v + eps)

def _scatter_add(tgt, idx, src, axis=0):
    return tgt.at[idx].add(src)

def _segment_sum(src, seg, n):
    return jax.ops.segment_sum(src, seg, n)
kernel_name = 'mk_adj_preln_d2_adj_r2_4b2689'

def setup_inputs(seed: int=0):
    np.random.seed(seed)
    _w = jnp.asarray

    def _rec_inputs():
        import jax
        import jax.numpy as jnp
        _gk = jax.random.key(seed)
        x = -0.000929 + 1 * jax.random.normal(jax.random.fold_in(_gk, 1), (4096, 128), jnp.float32)
        _a = jax.random.bernoulli(jax.random.fold_in(_gk, 2), 0.000976562, (4096, 4096))
        _a = jnp.logical_or(_a, jnp.swapaxes(_a, -1, -2))
        _a = jnp.logical_or(_a, jnp.eye(4096, dtype=bool))
        _af = _a.astype(jnp.float32)
        _af = _af * jax.random.uniform(jax.random.fold_in(_gk, 3), (4096, 4096), jnp.float32, 0.05, 1)
        adj = _af
        return (x, adj)
    x, adj = _rec_inputs()

    def _L0_gnn_setup():
        import jax, jax.numpy as jnp
        import numpy as np
        N = 4096
        F_IN = 128
        F_OUT = 128
        key = jax.random.key(seed)
        k1, k2, k3, k4, k5 = jax.random.split(key, 5)
        x = jax.random.normal(k1, (N, F_IN), dtype=jnp.float32)
        adj = jax.random.uniform(k2, (N, N), dtype=jnp.float32)
        kernel = jax.random.normal(k3, (F_IN, F_OUT), dtype=jnp.float32) * 0.05
        bias = jax.random.normal(k4, (F_OUT,), dtype=jnp.float32) * 0.05
        beta = jax.random.uniform(k5, (N,), dtype=jnp.float32)
        return {'x': x, 'adj': adj, 'kernel': kernel, 'bias': bias, 'beta': beta}
    _L0_gnn_all = _L0_gnn_setup()
    _L0_gnn_in = {k: v for k, v in _L0_gnn_all.items() if k in ('kernel', 'bias', 'beta')}
    del _L0_gnn_all

    def _L1_gnn_setup():
        import jax, jax.numpy as jnp
        import numpy as np
        import math
        N = 4096
        D_IN = 128
        H = 128
        GATE_TEMPERATURE = 1.0
        LN_EPS = 1e-05
        key = jax.random.key(seed)
        ks = jax.random.split(key, 10)
        s_msg = 1.0 / math.sqrt(D_IN)
        s_gate = 1.0 / math.sqrt(H)
        s_upd = 1.0 / math.sqrt(D_IN + H)
        return {'node_features': jax.random.normal(ks[0], (N, D_IN), dtype=jnp.float32), 'adj_matrix': jax.random.uniform(ks[1], (N, N), dtype=jnp.float32), 'recency_prior': jax.random.uniform(ks[2], (N, N), dtype=jnp.float32), 'W_msg': jax.random.uniform(ks[3], (D_IN, H), jnp.float32, -s_msg, s_msg), 'b_msg': jax.random.uniform(ks[4], (H,), jnp.float32, -s_msg, s_msg), 'W_q': jax.random.uniform(ks[5], (H, H), jnp.float32, -s_gate, s_gate), 'W_k': jax.random.uniform(ks[6], (H, H), jnp.float32, -s_gate, s_gate), 'gate_bias': jnp.float32(-1.0), 'W_upd': jax.random.uniform(ks[7], (D_IN + H, H), jnp.float32, -s_upd, s_upd), 'b_upd': jax.random.uniform(ks[8], (H,), jnp.float32, -s_upd, s_upd), 'ln_gamma': jnp.ones((H,), jnp.float32), 'ln_beta': jnp.zeros((H,), jnp.float32)}
    _L1_gnn_all = _L1_gnn_setup()
    _L1_gnn_in = {k: v for k, v in _L1_gnn_all.items() if k in ('W_msg', 'b_msg', 'W_q', 'W_k', 'gate_bias', 'W_upd', 'b_upd', 'ln_gamma', 'ln_beta')}
    del _L1_gnn_all
    return {'x': x, 'adj': adj, 'L0_gnn_kernel': _L0_gnn_in['kernel'], 'L0_gnn_bias': _L0_gnn_in['bias'], 'L0_gnn_beta': _L0_gnn_in['beta'], 'L1_gnn_W_msg': _L1_gnn_in['W_msg'], 'L1_gnn_b_msg': _L1_gnn_in['b_msg'], 'L1_gnn_W_q': _L1_gnn_in['W_q'], 'L1_gnn_W_k': _L1_gnn_in['W_k'], 'L1_gnn_gate_bias': _L1_gnn_in['gate_bias'], 'L1_gnn_W_upd': _L1_gnn_in['W_upd'], 'L1_gnn_b_upd': _L1_gnn_in['b_upd'], 'L1_gnn_ln_gamma': _L1_gnn_in['ln_gamma'], 'L1_gnn_ln_beta': _L1_gnn_in['ln_beta']}

def reference(x, adj, L0_gnn_kernel, L0_gnn_bias, L0_gnn_beta, L1_gnn_W_msg, L1_gnn_b_msg, L1_gnn_W_q, L1_gnn_W_k, L1_gnn_gate_bias, L1_gnn_W_upd, L1_gnn_b_upd, L1_gnn_ln_gamma, L1_gnn_ln_beta):
    import jax
    import jax.numpy as jnp

    def _L0_gnn_ref(x, adj, kernel, bias, beta):
        import jax, jax.numpy as jnp
        import numpy as np
        N = 4096
        F_IN = 128
        F_OUT = 128
        inv_deg = 1.0 / (jnp.sum(adj, axis=1) + beta)
        agg = adj @ x + beta[:, None] * x
        out = inv_deg[:, None] * agg @ kernel + bias
        return out

    def _L1_gnn_ref(node_features, adj_matrix, recency_prior, W_msg, b_msg, W_q, W_k, gate_bias, W_upd, b_upd, ln_gamma, ln_beta):
        import jax, jax.numpy as jnp
        import numpy as np
        import math
        N = 4096
        D_IN = 128
        H = 128
        GATE_TEMPERATURE = 1.0
        LN_EPS = 1e-05
        messages = node_features @ W_msg + b_msg
        q = messages @ W_q
        k = messages @ W_k
        scale = math.sqrt(H) * max(GATE_TEMPERATURE, 1e-06)
        logits = q @ k.T / scale + gate_bias
        probs = jax.nn.sigmoid(logits)
        gates_masked = probs * adj_matrix * recency_prior
        aggregated = gates_masked @ messages
        updated = jnp.concatenate([node_features, aggregated], axis=1) @ W_upd + b_upd
        updated = jax.nn.relu(updated)
        mu = jnp.mean(updated, axis=-1, keepdims=True)
        var = jnp.var(updated, axis=-1, keepdims=True)
        out = (updated - mu) * jax.lax.rsqrt(var + LN_EPS) * ln_gamma + ln_beta
        return out
    h = jnp.maximum(_layernorm(x, axis=-1), 0.0)
    x = x + _L0_gnn_ref(h, adj, L0_gnn_kernel, L0_gnn_bias, L0_gnn_beta)
    h = jnp.maximum(_layernorm(x, axis=-1), 0.0)
    x = x + _L1_gnn_ref(h, adj, adj, L1_gnn_W_msg, L1_gnn_b_msg, L1_gnn_W_q, L1_gnn_W_k, L1_gnn_gate_bias, L1_gnn_W_upd, L1_gnn_b_upd, L1_gnn_ln_gamma, L1_gnn_ln_beta)
    return x

_drawn_inputs = setup_inputs


def setup_inputs(seed=0):
    import zlib

    import numpy as np

    out = dict(_drawn_inputs(seed))
    spreads = {'L1_gnn_ln_gamma': (1.0, 0.2), 'L1_gnn_ln_beta': (0.0, 0.1)}
    factors = {'L0_gnn_beta': 3.051, 'L1_gnn_W_q': 7.15, 'L1_gnn_W_k': 6.244}
    for name, (base, spread) in spreads.items():
        noise = np.random.default_rng([zlib.crc32(name.encode()), seed]).standard_normal(out[name].shape)
        drawn = base * np.exp(spread * noise) if base else spread * noise
        out[name] = jnp.asarray(drawn.astype(out[name].dtype))
    for name, factor in factors.items():
        out[name] = (out[name] * factor).astype(out[name].dtype)
    return out
```

```python
import concourse.bass as bass
from concourse import mybir
from contextlib import ExitStack

P = 128
N = 4096
F = 128
CHUNKS = N // P
BLOCKS = 4
W = N // BLOCKS
HALF = 512
SUBS = HALF // P
PAIRS = CHUNKS // 2
RING = 4
GATE_RING = 4
SPLIT_RING = 2
LAG = 2
GROUP = 8
SPLIT_IN_GROUP = [3, 6]
NATIVE_IN_GROUP = [k for k in range(GROUP) if k not in SPLIT_IN_GROUP]
NS, NN = len(SPLIT_IN_GROUP), len(NATIVE_IN_GROUP)
SPLIT0 = [c for c in range(CHUNKS) if c % GROUP in SPLIT_IN_GROUP]
NATIVE0 = [c for c in range(CHUNKS) if c % GROUP in NATIVE_IN_GROUP]
NSPLIT = len(SPLIT0)
LN_EPS = 1e-5

F32 = mybir.dt.float32
F32R = mybir.dt.float32r
ALU = mybir.AluOpType
ACT = mybir.ActivationFunctionType

EPI_START = [1, 12]
(SL_PROJECT, SL_RESIDUAL, SL_SHIFT, SL_RELU, SL_TURN, SL_TURNED, SL_MESSAGE, SL_MSG_COPY,
 SL_MSG_LO, SL_MSG_TURN, SL_M_HI, SL_M_LO) = 0, 1, 2, 3, 4, 5, 6, 7, 8, 8, 9, 10
FIN_START = [2, 12]
(SL_UPDATE, SL_SUM, SL_FRELU, SL_FSTATS, SL_FSHIFT, SL_FNORM) = 1, 2, 3, 4, 6, 7
SL_Q, SL_Q_HI, SL_Q_LO = 24, 25, 26


def gnn_kernel(nc, x, adj_t, weights, rows, cols, out):
    ctx = ExitStack()
    with ctx:
        def sb(name, shape, dt=F32):
            return ctx.enter_context(nc.sbuf_tensor(name, shape, dt))

        def pb(name, shape):
            return ctx.enter_context(nc.psum_tensor(name, shape, F32))

        def sem(name):
            return ctx.enter_context(nc.semaphore(name))

        adj = sb("adj", [P, RING, 2, W])
        gate = sb("gate", [P, GATE_RING, W])
        tile_hi = sb("tile_hi", [P, SPLIT_RING, W], F32R)
        tile_lo = sb("tile_lo", [P, SPLIT_RING, W], F32R)
        deg_sum = gate[:, 2, :]
        deg_block = gate[:, 3, :]
        h_f32 = sb("h_f32", [P, len(NATIVE0), F])
        hq_hi = sb("hq_hi", [P, 2 * W], F32R)
        hq_lo = sb("hq_lo", [P, 2 * W], F32R)
        x1 = sb("x1", [P, CHUNKS, F])
        u1 = sb("u1", [P, CHUNKS, F])
        msg_hi = sb("msg_hi", [P, CHUNKS, F], F32R)
        msg_lo = sb("msg_lo", [P, CHUNKS, F], F32R)
        msgt_hi = sb("msgt_hi", [P, N], F32R)
        msgt_lo = sb("msgt_lo", [P, N], F32R)
        agg_sb = sb("agg_sb", [P, W])
        node_a = sb("node_a", [P, SUBS, F])
        node_b = sb("node_b", [P, HALF])
        msgt_f = sb("msgt_f", [P, HALF])
        w_sb = sb("w_sb", [P, 6, F])
        W0, WMSG, WU_H, WU_A, WQ_T, WK_T = (w_sb[:, k, :] for k in range(6))
        rows_sb = sb("rows_sb", [P, 4 * F + 1])
        BIAS0, B_UPD, GAMMA, BETA_LN = (rows_sb[:, k * F:(k + 1) * F] for k in range(4))
        GATE_BIAS = rows_sb[:, 4 * F:4 * F + 1]
        cols_sb = sb("cols_sb", [P, CHUNKS + 1])
        B_MSG = cols_sb[:, CHUNKS:CHUNKS + 1]
        g_hi = sb("g_hi", [P, F], F32R)
        g_lo = sb("g_lo", [P, F], F32R)
        ident = sb("ident", [P, P])
        ones = sb("ones", [P, 1])
        minus_half = sb("minus_half", [P, GROUP])
        eps = sb("eps", [P, GROUP])
        stats = sb("stats", [P, GROUP, 6])
        mean_var = sb("mean_var", [P, GROUP, 2])
        var_eps = sb("var_eps", [P, GROUP])
        rstd = sb("rstd", [P, GROUP])
        shift = sb("shift", [P, GROUP])
        inv_deg = sb("inv_deg", [P, W // P])

        agg_ps = pb("agg_ps", [P, W])
        logit_ps = pb("logit_ps", [P, 2, W])
        scr = pb("scr", [P, W])
        SCR0, SCR1 = scr[:, 0:HALF], scr[:, HALF:W]

        x_landed = [sem(f"x_landed{g}") for g in range(CHUNKS // GROUP)]
        w_landed = sem("w_landed")
        rows_landed = sem("rows_landed")
        cols_landed = sem("cols_landed")
        adj_landed = [sem(f"adj_landed{r}") for r in range(RING)]
        consts_ready = sem("consts_ready")
        ident_zeroed = sem("ident_zeroed")
        ident_ready = sem("ident_ready")
        bn_done = sem("bn_done")
        stats_ready = sem("stats_ready")
        eps_added = sem("eps_added")
        rstd_ready = sem("rstd_ready")
        shift_ready = sem("shift_ready")
        h_ready = sem("h_ready")
        h_hi_ready = sem("h_hi_ready")
        h_lo_ready = sem("h_lo_ready")
        bias_added = sem("bias_added")
        g_ready = sem("g_ready")
        g_hi_ready = sem("g_hi_ready")
        g_lo_ready = sem("g_lo_ready")
        diag_added = sem("diag_added")
        deg_added = sem("deg_added")
        adj_hi_ready = sem("adj_hi_ready")
        adj_lo_ready = sem("adj_lo_ready")
        adj_used = sem("adj_used")
        sum_copied = sem("sum_copied")
        projected = sem("projected")
        inv_ready = sem("inv_ready")
        x1_ready = sem("x1_ready")
        h2_ready = sem("h2_ready")
        h2_turned = sem("h2_turned")
        h2t_ready = sem("h2t_ready")
        msgt_ready = sem("msgt_ready")
        msgt_copied = sem("msgt_copied")
        u1_ready = sem("u1_ready")
        msgt_split = sem("msgt_split")
        msg_turned = sem("msg_turned")
        msg_hi_ready = sem("msg_hi_ready")
        msg_split = sem("msg_split")
        q_ready = sem("q_ready")
        q_hi_ready = sem("q_hi_ready")
        q_lo_ready = sem("q_lo_ready")
        logit_ready = sem("logit_ready")
        sig_ready = sem("sig_ready")
        squared = sem("squared")
        gate_ready = sem("gate_ready")
        gate_hi_ready = sem("gate_hi_ready")
        gate_lo_ready = sem("gate_lo_ready")
        gate_used = sem("gate_used")
        updated = sem("updated")
        summed = sem("summed")
        frelu_ready = sem("frelu_ready")
        norm_ready = sem("norm_ready")
        scaled = sem("scaled")
        out_stored = sem("out_stored")

        N_GROUPS = CHUNKS // GROUP
        HALVES = 2 * BLOCKS

        def sub(ap, e):
            return ap[:, e * P:(e + 1) * P]

        def half(ap, k):
            return ap[:, k * HALF:(k + 1) * HALF]

        def h_split(c, part):
            return part[:, SPLIT0.index(c) * F:(SPLIT0.index(c) + 1) * F]

        def half_nodes(ap, b, hb):
            return ap[:, bass.ds(b * (W // P) + hb * SUBS, SUBS), :]

        def half_cols(ap, b, hb):
            return ap[:, bass.ds(b * W + hb * HALF, HALF)]

        def pair_of(c):
            return (c // 2) % RING

        def landed(eng, layer, b, c):
            eng.wait_ge(adj_landed[pair_of(c)],
                        (b + layer * BLOCKS) * (16 * PAIRS // RING) + 16 * (c // 2 // RING + 1))

        def prev(b, c, back, first):
            if first and c < back:
                return None
            return b * CHUNKS + (c - back + 1)

        block = ctx.enter_context(nc.Block())

        @block.sync
        def _(sp):
            for g in range(N_GROUPS):
                sp.dma_start(x1[:, g * GROUP:(g + 1) * GROUP, :], x[g]).then_inc(x_landed[g], 16)

            def load(layer, b, p, first=False):
                done = b * CHUNKS + 2 * (p - RING) + 2
                if first and p < RING:
                    if layer == 1:
                        sp.wait_ge(adj_used, BLOCKS * CHUNKS + done)
                elif layer == 0:
                    sp.wait_ge(adj_used, done)
                else:
                    sp.wait_ge(gate_ready, done)
                src = adj_t[bass.ds(b, 1), p].rearrange("o p g i -> (o p) g i")
                sp.dma_start(adj[:, p % RING, :, :], src).then_inc(adj_landed[p % RING], 16)

            for p in range(PAIRS):
                load(0, 0, p, first=True)
            with sp.Fori(1, BLOCKS) as b:
                for p in range(PAIRS):
                    load(0, b, p)
            for p in range(PAIRS):
                load(1, 0, p, first=True)

            def store(b, hb):
                sp.wait_ge(scaled, 3 * (2 * b + hb + 1))
                dst = out[bass.ds(2 * b + hb, 1)].rearrange("o p n -> (o p) n")
                sp.dma_start(dst, node_b[:, :]).then_inc(out_stored, 16)

            with sp.Fori(1, BLOCKS) as b:
                for p in range(PAIRS):
                    load(1, b, p)
                    for hb in range(2):
                        if p == (FIN_START[hb] + SL_FNORM) // 2 + RING:
                            store(b - 1, hb)
            for hb in range(2):
                store(BLOCKS - 1, hb)
            sp.wait_ge(out_stored, 16 * HALVES)

        @block.tensor
        def _(pe):
            def split_products(dst, w_hi, w_lo, m_hi, m_lo, start, stop, before_lo=None):
                for k, (wt, mv) in enumerate([(w_hi, m_hi), (w_lo, m_hi), (w_hi, m_lo)]):
                    if k == 2 and before_lo is not None:
                        before_lo()
                    for hf in range(2):
                        mm = pe.matmul(half(dst, hf), wt, mv(hf), start=start and k == 0, stop=stop and k == 2)
                return mm

            pe.wait_ge(w_landed, 16)
            pe.matmul(SCR0[:, 0:F], WQ_T, WK_T, start=True, stop=True).then_inc(g_ready, 1)

            def tile0(b, c, first):
                if first and c % GROUP == 0:
                    pe.wait_ge(h_ready, c // GROUP + 1)
                    pe.wait_ge(h_lo_ready, c // GROUP + 1)
                start, stop = c == 0, c == CHUNKS - 1
                if c in NATIVE0:
                    pe.wait_ge(deg_added, b * (CHUNKS - 1) + max(c, 1))
                    for hf in range(2):
                        if start and not first:
                            pe.wait_ge(sum_copied, 2 * (b - 1) + hf + 1)
                        mm = pe.matmul(half(agg_ps, hf), h_f32[:, NATIVE0.index(c), :],
                                       half(adj[:, pair_of(c), c % 2, :], hf), start=start, stop=stop)
                else:
                    s = SPLIT0.index(c)
                    pe.wait_ge(adj_hi_ready, b * NSPLIT + s + 1)
                    mm = split_products(agg_ps, h_split(c, hq_hi), h_split(c, hq_lo),
                                        lambda hf: half(tile_hi[:, s % SPLIT_RING, :], hf),
                                        lambda hf: half(tile_lo[:, s % SPLIT_RING, :], hf), start, stop,
                                        lambda: pe.wait_ge(adj_lo_ready, b * NSPLIT + s + 1))
                mm.then_inc(adj_used, 1)

            def epilogue0(b, slot):
                for hb in range(2):
                    at, r = slot - EPI_START[hb], 2 * b + hb
                    if at == SL_PROJECT:
                        pe.wait_ge(sum_copied, 2 * b + 2)
                        if hb == 0:
                            pe.wait_ge(deg_added, (b + 1) * (CHUNKS - 1))
                        if not (isinstance(b, int) and b == 0 and hb == 0):
                            pe.wait_ge(msg_split, r)
                            pe.wait_ge(msgt_copied, 2 * r)
                        else:
                            pe.wait_ge(g_lo_ready, 1)
                        if hb == 0:
                            for e in range(W // P):
                                pe.matmul(SCR1[:, e:e + 1], sub(deg_block, e), ones[:, 0:1], start=True, stop=True)
                        for e in range(SUBS):
                            mm = pe.matmul(sub(SCR0, e), sub(agg_sb, hb * SUBS + e), W0, start=True, stop=True)
                        mm.then_inc(projected, 1)
                    if at == SL_TURN:
                        pe.wait_ge(h2_ready, r + 1)
                        for e in range(SUBS):
                            mm = pe.transpose(sub(SCR0, e), node_a[:, e, :], ident[:, :])
                        mm.then_inc(h2_turned, 1)
                    if at == SL_MESSAGE:
                        pe.wait_ge(h2t_ready, r + 1)
                        pe.matmul(SCR1, WMSG, node_b[:, :], start=True, stop=True).then_inc(msgt_ready, 1)
                        for e in range(SUBS):
                            mm = pe.matmul(sub(SCR0, e), sub(node_b, e), WU_H, start=True, stop=True)
                        mm.then_inc(msgt_ready, 1)
                    if at == SL_MSG_TURN:
                        pe.wait_ge(u1_ready, r + 1)
                        pe.wait_ge(msgt_copied, 2 * (r + 1))
                        for e in range(SUBS):
                            mm = pe.transpose(sub(SCR0, e), sub(msgt_f, e), ident[:, :])
                        mm.then_inc(msg_turned, 1)

            def query(b_next):
                for k, (wt, mv) in enumerate([(g_hi, msgt_hi), (g_lo, msgt_hi), (g_hi, msgt_lo)]):
                    for hf in range(2):
                        mm = pe.matmul(half(scr, hf), wt[:, :], half_cols(mv, b_next, hf), start=k == 0, stop=k == 2)
                mm.then_inc(q_ready, 1)

            def logits(b, c, first):
                if c == 0:
                    pe.wait_ge(q_lo_ready, b + 1)
                if first and c in (0, 24, 28):
                    pe.wait_ge(msgt_split, HALVES if c == 28 else HALVES - 1 if c == 24 else HALVES - 2)
                free = prev(b, c, 2, first)
                if free is not None:
                    pe.wait_ge(sig_ready, free)
                par = b % 2
                split_products(logit_ps[:, c % 2, :], sub(msgt_hi, c), sub(msgt_lo, c),
                               lambda hf: half_cols(hq_hi, par, hf),
                               lambda hf: half_cols(hq_lo, par, hf), True, True).then_inc(logit_ready, 1)

            def aggregate(b, c, first):
                t = b * CHUNKS + c
                if c == 0:
                    pe.wait_ge(sum_copied, 2 * (BLOCKS + b))
                if first and c in (0, 24, 28):
                    pe.wait_ge(msg_split, HALVES if c == 28 else HALVES - 1 if c == 24 else HALVES - 2)
                pe.wait_ge(gate_hi_ready, t + 1)
                split_products(agg_ps, msg_hi[:, c, :], msg_lo[:, c, :],
                               lambda hf: half(tile_hi[:, c % SPLIT_RING, :], hf),
                               lambda hf: half(tile_lo[:, c % SPLIT_RING, :], hf), c == 0, c == CHUNKS - 1,
                               lambda: pe.wait_ge(gate_lo_ready, t + 1)).then_inc(gate_used, 1)

            def epilogue1(b, slot):
                for hb in range(2):
                    at, r = slot - FIN_START[hb], 2 * b + hb
                    if at == SL_UPDATE:
                        pe.wait_ge(sum_copied, 2 * (BLOCKS + b + 1))
                        pe.wait_ge(q_lo_ready, b + 2)
                        if hb:
                            pe.wait_ge(summed, r)
                        for e in range(SUBS):
                            mm = pe.matmul(sub(SCR0, e), sub(agg_sb, hb * SUBS + e), WU_A, start=True, stop=True)
                        mm.then_inc(updated, 1)

            for c in range(CHUNKS):
                tile0(0, c, True)
            pe.wait_ge(ident_ready, 1)
            with pe.Fori(1, BLOCKS) as b:
                for c in range(CHUNKS):
                    tile0(b, c, False)
                    epilogue0(b - 1, c)
            pe.wait_ge(msg_split, HALVES - 2)
            query(0)
            for c in range(CHUNKS):
                logits(0, c, True)
                if c >= LAG:
                    aggregate(0, c - LAG, True)
                epilogue0(BLOCKS - 1, c)
                if c == SL_Q:
                    pe.wait_ge(msg_split, HALVES)
                    query(1)
            with pe.Fori(1, BLOCKS) as b:
                for c in range(CHUNKS):
                    logits(b, c, False)
                    if c >= LAG:
                        aggregate(b, c - LAG, False)
                    else:
                        aggregate(b - 1, CHUNKS - LAG + c, False)
                    epilogue1(b - 1, c)
                    if c == SL_Q:
                        pe.wait_ge(summed, 2 * b)
                        query((b + 1) % BLOCKS)
            for c in range(CHUNKS - LAG, CHUNKS):
                aggregate(BLOCKS - 1, c, False)
            for slot in range(CHUNKS):
                epilogue1(BLOCKS - 1, slot)

        @block.scalar
        def _(act):
            act.dma_start(rows_sb[:, :], rows.partition_broadcast(P)).then_inc(rows_landed, 16)
            act.dma_start(cols_sb[:, :], cols).then_inc(cols_landed, 16)
            act.dma_start(w_sb[:, :, :], weights).then_inc(w_landed, 16)

            for g in range(N_GROUPS):
                act.wait_ge(shift_ready, g + 1)
                for k in range(GROUP):
                    c = g * GROUP + k
                    dst = (h_f32[:, NATIVE0.index(c), :] if c in NATIVE0
                           else u1[:, g * NS + SPLIT_IN_GROUP.index(k), :])
                    i = act.activation(dst, x1[:, c, :], ACT.Relu, bias=shift[:, k:k + 1], scale=rstd[:, k:k + 1])
                i.then_inc(h_ready, 1)
                act.wait_ge(h_ready, g + 1)
                act.activation(hq_hi[:, g * NS * F:(g + 1) * NS * F],
                               u1[:, g * NS:(g + 1) * NS, :].rearrange("p a f -> p (a f)"),
                               ACT.Copy).then_inc(h_hi_ready, 1)
            act.wait_ge(g_ready, 1)
            act.activation(g_hi[:, :], SCR0[:, 0:F], ACT.Copy).then_inc(g_hi_ready, 1)

            def adj_hi(b, c, first):
                s = SPLIT0.index(c)
                act.wait_ge(deg_added, b * (CHUNKS - 1) + c)
                if not (first and s < SPLIT_RING):
                    before = SPLIT0[s - SPLIT_RING] if s >= SPLIT_RING else SPLIT0[s - SPLIT_RING] - CHUNKS
                    act.wait_ge(adj_used, b * CHUNKS + before + 1)
                act.activation(tile_hi[:, s % SPLIT_RING, :], adj[:, pair_of(c), c % 2, :],
                               ACT.Copy).then_inc(adj_hi_ready, 1)

            def copy_sums(done, count, halves=(0, 1)):
                act.wait_ge(done, count)
                for hf in halves:
                    act.activation(half(agg_sb, hf), half(agg_ps, hf), ACT.Copy).then_inc(sum_copied, 1)

            def epilogue0(b, slot):
                for hb in range(2):
                    at, r = slot - EPI_START[hb], 2 * b + hb
                    if at == SL_RELU:
                        act.wait_ge(shift_ready, N_GROUPS + r + 1)
                        for e in range(SUBS):
                            i = act.activation(node_a[:, e, :], x1[:, bass.ds(b * (W // P) + hb * SUBS + e, 1), :],
                                               ACT.Relu, bias=shift[:, e:e + 1], scale=rstd[:, e:e + 1])
                        i.then_inc(h2_ready, 1)
                    if at == SL_TURNED:
                        act.wait_ge(h2_turned, r + 1)
                        act.activation(node_b[:, :], SCR0, ACT.Copy).then_inc(h2t_ready, 1)
                    if at == SL_MSG_COPY:
                        act.wait_ge(msgt_ready, 2 * r + 1)
                        act.activation(msgt_f[:, :], SCR1, ACT.Identity, bias=B_MSG).then_inc(msgt_copied, 1)
                        act.activation(half_cols(msgt_hi, b, hb), SCR1, ACT.Identity,
                                       bias=B_MSG).then_inc(msgt_copied, 1)
                    if at == SL_M_HI:
                        act.wait_ge(msg_turned, r + 1)
                        act.activation(half_nodes(msg_hi, b, hb),
                                       SCR0.rearrange("p (a f) -> p a f", a=SUBS), ACT.Copy).then_inc(msg_hi_ready, 1)

            def q_hi(b_next):
                act.wait_ge(q_ready, b_next + 1)
                act.activation(hq_hi[:, bass.ds((b_next % 2) * W, W)], scr[:, :], ACT.Copy).then_inc(q_hi_ready, 1)

            def square(b, c):
                landed(act, 1, b, c)
                pair = adj[:, pair_of(c), :, :]
                act.activation(pair, pair, ACT.Square).then_inc(squared, 1)

            def sigmoid(b, c, first):
                act.wait_ge(logit_ready, b * CHUNKS + c + 1)
                free = prev(b, c, GATE_RING, first)
                if free is not None:
                    act.wait_ge(gate_lo_ready, free)
                if first and c == 3:
                    act.wait_ge(projected, HALVES - 1)
                act.activation(gate[:, c % GATE_RING, :], logit_ps[:, c % 2, :], ACT.Sigmoid,
                               bias=GATE_BIAS, scale=float(F) ** -0.5).then_inc(sig_ready, 1)

            def gate_hi(b, c, first):
                act.wait_ge(gate_ready, b * CHUNKS + c + 1)
                free = prev(b, c, SPLIT_RING, first)
                if free is not None:
                    act.wait_ge(gate_used, free)
                act.activation(tile_hi[:, c % SPLIT_RING, :], gate[:, c % GATE_RING, :],
                               ACT.Copy).then_inc(gate_hi_ready, 1)

            def epilogue1(b, slot):
                for hb in range(2):
                    at, r = slot - FIN_START[hb], 2 * b + hb
                    if at == SL_FRELU:
                        act.wait_ge(summed, r + 1)
                        act.activation(node_a[:, :, :], node_a[:, :, :], ACT.Relu).then_inc(frelu_ready, 1)
                    if at == SL_FNORM:
                        act.wait_ge(shift_ready, N_GROUPS + HALVES + r + 1)
                        if not (isinstance(b, int) and b == 0 and hb == 0):
                            act.wait_ge(out_stored, 16 * r)
                        for e in range(SUBS):
                            i = act.activation(sub(node_b, e), node_a[:, e, :], ACT.Identity,
                                               bias=shift[:, e:e + 1], scale=rstd[:, e:e + 1])
                        i.then_inc(norm_ready, 1)

            for c in SPLIT0:
                adj_hi(0, c, True)
            with act.Fori(1, BLOCKS) as b:
                copy_sums(adj_used, b * CHUNKS)
                for c in range(CHUNKS):
                    if c in SPLIT0:
                        adj_hi(b, c, False)
                    epilogue0(b - 1, c)
            copy_sums(adj_used, BLOCKS * CHUNKS)
            act.wait_ge(rows_landed, 16)
            q_hi(0)
            square(0, 0)
            for c in range(CHUNKS):
                sigmoid(0, c, True)
                if c >= 1:
                    gate_hi(0, c - 1, True)
                if c % 2 == 0 and c + 2 < CHUNKS:
                    square(0, c + 2)
                epilogue0(BLOCKS - 1, c)
                if c == SL_Q_HI:
                    q_hi(1)
            with act.Fori(1, BLOCKS) as b:
                for c in range(CHUNKS):
                    if c == 0:
                        square(b, 0)
                    sigmoid(b, c, False)
                    if c >= 1:
                        gate_hi(b, c - 1, False)
                    else:
                        gate_hi(b - 1, CHUNKS - 1, False)
                    if c == LAG - 1:
                        copy_sums(gate_used, b * CHUNKS)
                    if c % 2 == 0 and c + 2 < CHUNKS:
                        square(b, c + 2)
                    epilogue1(b - 1, c)
                    if c == SL_Q_HI:
                        q_hi(b + 1)
            gate_hi(BLOCKS - 1, CHUNKS - 1, False)
            copy_sums(gate_used, BLOCKS * CHUNKS)
            for slot in range(CHUNKS):
                epilogue1(BLOCKS - 1, slot)

        @block.vector
        def _(dve):
            dve.memset(ones[:, :], 1.0).then_inc(consts_ready, 1)
            dve.memset(minus_half[:, :], -0.5).then_inc(consts_ready, 1)
            dve.memset(eps[:, :], LN_EPS).then_inc(consts_ready, 1)

            def partial_stats(parts):
                for k, part in enumerate(parts):
                    i = dve.bn_stats(stats[:, k, :], part)
                i.then_inc(bn_done, 1)

            def whole_stats(rows_n):
                for k in range(rows_n):
                    i = dve.bn_aggr(mean_var[:, k, :], stats[:, k, :])
                i.then_inc(stats_ready, 1)

            def layer_stats(parts, n):
                partial_stats(parts)
                dve.wait_ge(bn_done, n + 1)
                whole_stats(len(parts))

            def layer_shift(rows_n, n):
                dve.wait_ge(rstd_ready, n + 1)
                dve.scalar_tensor_tensor(out=shift[:, 0:rows_n], in0=mean_var[:, 0:rows_n, 0], scalar=-1.0,
                                         in1=rstd[:, 0:rows_n], op0=ALU.mult, op1=ALU.mult).then_inc(shift_ready, 1)

            for g in range(N_GROUPS):
                dve.wait_ge(x_landed[g], 16)
                if g:
                    dve.wait_ge(shift_ready, g)
                layer_stats([x1[:, g * GROUP + k, :] for k in range(GROUP)], g)
                if g:
                    dve.wait_ge(h_ready, g)
                layer_shift(GROUP, g)
                dve.wait_ge(h_hi_ready, g + 1)
                cols_g = slice(g * NS * F, (g + 1) * NS * F)
                dve.tensor_tensor(hq_lo[:, cols_g], u1[:, g * NS:(g + 1) * NS, :].rearrange("p a f -> p (a f)"),
                                  hq_hi[:, cols_g].bitcast(F32), ALU.subtract).then_inc(h_lo_ready, 1)
            dve.wait_ge(g_hi_ready, 1)
            dve.tensor_tensor(g_lo[:, :], SCR0[:, 0:F], g_hi[:, :].bitcast(F32), ALU.subtract).then_inc(g_lo_ready, 1)
            dve.wait_ge(cols_landed, 16)
            dve.wait_ge(ident_ready, 1)

            def add_degree(b, c):
                landed(dve, 0, b, c)
                here = adj[:, pair_of(c), c % 2, :]
                if c // (W // P) == b:
                    e = c % (W // P)
                    dve.scalar_tensor_tensor(out=sub(here, e), in0=ident[:, :], scalar=cols_sb[:, c:c + 1],
                                             in1=sub(here, e), op0=ALU.mult, op1=ALU.add).then_inc(diag_added, 1)
                    dve.wait_ge(diag_added, c + 1)
                if c == 0:
                    return
                before = adj[:, pair_of(0), 0, :] if c == 1 else deg_sum
                if b or c > 1:
                    dve.wait_ge(deg_added, b * (CHUNKS - 1) + c - 1)
                dst = deg_sum if c < CHUNKS - 1 else deg_block
                if c == CHUNKS - 1 and b > 0:
                    dve.wait_ge(projected, 2 * b - 1)
                dve.tensor_tensor(dst, before, here, ALU.add).then_inc(deg_added, 1)

            def adj_lo(b, c):
                s = SPLIT0.index(c)
                dve.wait_ge(adj_hi_ready, b * NSPLIT + s + 1)
                dve.tensor_tensor(tile_lo[:, s % SPLIT_RING, :], adj[:, pair_of(c), c % 2, :],
                                  tile_hi[:, s % SPLIT_RING, :].bitcast(F32), ALU.subtract).then_inc(adj_lo_ready, 1)

            def epilogue0(b, slot):
                for hb in range(2):
                    at, r = slot - EPI_START[hb], 2 * b + hb
                    if at == SL_RESIDUAL:
                        dve.wait_ge(projected, r + 1)
                        if hb == 0:
                            dve.reciprocal(inv_deg[:, :], SCR1[:, 0:W // P]).then_inc(inv_ready, 1)
                            dve.wait_ge(inv_ready, b + 1)
                            if b == 0:
                                dve.wait_ge(bias_added, 1)
                        for e in range(SUBS):
                            c = b * (W // P) + hb * SUBS + e
                            i = dve.scalar_tensor_tensor(
                                out=x1[:, c, :], in0=sub(SCR0, e), scalar=inv_deg[:, hb * SUBS + e:hb * SUBS + e + 1],
                                in1=x1[:, c, :], op0=ALU.mult, op1=ALU.add)
                        i.then_inc(x1_ready, 1)
                        dve.wait_ge(x1_ready, r + 1)
                        layer_stats([x1[:, b * (W // P) + hb * SUBS + e, :] for e in range(SUBS)], N_GROUPS + r)
                    if at == SL_SHIFT:
                        layer_shift(SUBS, N_GROUPS + r)
                    if at == SL_MSG_COPY:
                        dve.wait_ge(msgt_ready, 2 * r + 2)
                        dve.tensor_tensor(half_nodes(u1, b, hb), SCR0.rearrange("p (a f) -> p a f", a=SUBS),
                                          B_UPD.unsqueeze(1).broadcast_to([P, SUBS, F]), ALU.add).then_inc(u1_ready, 1)
                    if at == SL_MSG_LO:
                        dve.wait_ge(msgt_copied, 2 * (r + 1))
                        dve.tensor_tensor(half_cols(msgt_lo, b, hb), msgt_f[:, :],
                                          half_cols(msgt_hi, b, hb).bitcast(F32), ALU.subtract).then_inc(msgt_split, 1)
                    if at == SL_M_LO:
                        dve.wait_ge(msg_hi_ready, r + 1)
                        dve.tensor_tensor(half_nodes(msg_lo, b, hb), SCR0.rearrange("p (a f) -> p a f", a=SUBS),
                                          half_nodes(msg_hi, b, hb).bitcast(F32), ALU.subtract).then_inc(msg_split, 1)

            def q_lo(b_next):
                dve.wait_ge(q_hi_ready, b_next + 1)
                at = bass.ds((b_next % 2) * W, W)
                dve.tensor_tensor(hq_lo[:, at], scr[:, :], hq_hi[:, at].bitcast(F32),
                                  ALU.subtract).then_inc(q_lo_ready, 1)

            def gates(b, c):
                t = b * CHUNKS + c
                dve.wait_ge(squared, b * PAIRS + c // 2 + 1)
                dve.wait_ge(sig_ready, t + 1)
                g = gate[:, c % GATE_RING, :]
                dve.tensor_tensor(g, g, adj[:, pair_of(c), c % 2, :], ALU.mult).then_inc(gate_ready, 1)

            def stats_wait(b, slot):
                for hb in range(2):
                    if slot == FIN_START[hb] + SL_FSTATS + 1:
                        dve.wait_ge(bn_done, N_GROUPS + HALVES + 2 * b + hb + 1)

            def gate_lo(b, c):
                dve.wait_ge(gate_hi_ready, b * CHUNKS + c + 1)
                dve.tensor_tensor(tile_lo[:, c % SPLIT_RING, :], gate[:, c % GATE_RING, :],
                                  tile_hi[:, c % SPLIT_RING, :].bitcast(F32), ALU.subtract).then_inc(gate_lo_ready, 1)

            def epilogue1(b, slot):
                for hb in range(2):
                    at, r = slot - FIN_START[hb], 2 * b + hb
                    if at == SL_SUM:
                        dve.wait_ge(updated, r + 1)
                        if not (isinstance(b, int) and b == 0 and hb == 0):
                            dve.wait_ge(norm_ready, r)
                        dve.tensor_tensor(node_a[:, :, :], SCR0.rearrange("p (a f) -> p a f", a=SUBS),
                                          half_nodes(u1, b, hb), ALU.add).then_inc(summed, 1)
                    if at == SL_FSTATS:
                        dve.wait_ge(frelu_ready, r + 1)
                        partial_stats([node_a[:, e, :] for e in range(SUBS)])
                        if isinstance(b, int):
                            dve.wait_ge(bn_done, N_GROUPS + HALVES + r + 1)
                            whole_stats(SUBS)
                    if at == SL_FSTATS + 1 and not isinstance(b, int):
                        whole_stats(SUBS)
                    if at == SL_FSHIFT:
                        layer_shift(SUBS, N_GROUPS + HALVES + r)

            for b in range(BLOCKS):
                for c in range(CHUNKS):
                    add_degree(b, c)
                    if c - 1 in SPLIT0:
                        adj_lo(b, c - 1)
                    if b:
                        epilogue0(b - 1, c)
            q_lo(0)
            for c in range(CHUNKS):
                gates(0, c)
                if c >= 1:
                    gate_lo(0, c - 1)
                epilogue0(BLOCKS - 1, c)
                if c == SL_Q_LO:
                    q_lo(1)
            with dve.Fori(1, BLOCKS) as b:
                for c in range(CHUNKS):
                    stats_wait(b - 1, c)
                    gates(b, c)
                    if c >= 1:
                        gate_lo(b, c - 1)
                    else:
                        gate_lo(b - 1, CHUNKS - 1)
                    epilogue1(b - 1, c)
                    if c == SL_Q_LO:
                        q_lo(b + 1)
            gate_lo(BLOCKS - 1, CHUNKS - 1)
            for slot in range(CHUNKS):
                epilogue1(BLOCKS - 1, slot)

        @block.gpsimd
        def _(pool):
            pool.memset(ident[:, :], 0.0).then_inc(ident_zeroed, 1)
            pool.wait_ge(ident_zeroed, 1)
            pool.affine_select(out=ident[:, :], in_=ident[:, :], compare_op=ALU.not_equal, fill=1.0, base=0,
                               pattern=[[-1, P]], channel_multiplier=1).then_inc(ident_ready, 1)
            pool.wait_ge(consts_ready, 3)

            def inv_std(rows_n, n):
                pool.wait_ge(stats_ready, n + 1)
                pool.tensor_tensor(var_eps[:, 0:rows_n], mean_var[:, 0:rows_n, 1], eps[:, 0:rows_n],
                                   ALU.add).then_inc(eps_added, 1)
                pool.wait_ge(eps_added, n + 1)
                pool.tensor_tensor(rstd[:, 0:rows_n], var_eps[:, 0:rows_n], minus_half[:, 0:rows_n],
                                   ALU.pow).then_inc(rstd_ready, 1)

            for g in range(N_GROUPS):
                if g:
                    pool.wait_ge(h_ready, g)
                inv_std(GROUP, g)
            pool.wait_ge(rows_landed, 16)
            pool.wait_ge(h_ready, N_GROUPS)
            pool.tensor_tensor(x1[:, :, :], x1[:, :, :], BIAS0.unsqueeze(1).broadcast_to([P, CHUNKS, F]),
                               ALU.add).then_inc(bias_added, 1)
            with pool.Fori(0, HALVES) as r:
                inv_std(SUBS, N_GROUPS + r)
            with pool.Fori(0, HALVES) as r:
                inv_std(SUBS, N_GROUPS + HALVES + r)
                y = node_b[:, :].rearrange("p (a f) -> p a f", a=SUBS)
                pool.wait_ge(norm_ready, r + 1)
                pool.tensor_tensor(y, y, GAMMA.unsqueeze(1).broadcast_to([P, SUBS, F]), ALU.mult).then_inc(scaled, 1)
                pool.wait_ge(scaled, 3 * r + 1)
                pool.tensor_tensor(y, y, BETA_LN.unsqueeze(1).broadcast_to([P, SUBS, F]), ALU.add).then_inc(scaled, 1)
                pool.wait_ge(scaled, 3 * r + 2)
                pool.tensor_tensor(y, y, x1[:, bass.ds(r * SUBS, SUBS), :], ALU.add).then_inc(scaled, 1)


def kernel(x, adj, L0_gnn_kernel, L0_gnn_bias, L0_gnn_beta, L1_gnn_W_msg, L1_gnn_b_msg, L1_gnn_W_q, L1_gnn_W_k,
           L1_gnn_gate_bias, L1_gnn_W_upd, L1_gnn_b_upd, L1_gnn_ln_gamma, L1_gnn_ln_beta):
    import numpy as _np
    import concourse.bacc as _bacc
    from concourse import mybir as _mybir
    from concourse.bass_utils import run_bass_kernel_spmd as _run

    a = _np.asarray
    groups = CHUNKS // GROUP
    arrays = {
        "in_x": a(x).reshape(groups, GROUP, P, F).transpose(0, 2, 1, 3),
        "in_adj_t": a(adj).reshape(BLOCKS, W, PAIRS, 2, P).transpose(0, 2, 4, 3, 1),
        "in_weights": _np.stack([a(L0_gnn_kernel), a(L1_gnn_W_msg), a(L1_gnn_W_upd)[:F], a(L1_gnn_W_upd)[F:],
                                 a(L1_gnn_W_q).T, a(L1_gnn_W_k).T], axis=1),
        "in_rows": _np.concatenate([a(L0_gnn_bias), a(L1_gnn_b_upd), a(L1_gnn_ln_gamma), a(L1_gnn_ln_beta),
                                    a(L1_gnn_gate_bias).reshape(1)]),
        "in_cols": _np.concatenate([a(L0_gnn_beta).reshape(CHUNKS, P).T, a(L1_gnn_b_msg).reshape(P, 1)], axis=1),
    }
    arrays = {k: _np.ascontiguousarray(v) for k, v in arrays.items()}
    nc = _bacc.Bacc("TRN2", target_bir_lowering=False, num_devices=1)
    args = [nc.dram_tensor(k, v.shape, _mybir.dt.from_np(v.dtype), kind="ExternalInput").ap()
            for k, v in arrays.items()]
    out = nc.dram_tensor("out_0", (2 * BLOCKS, P, HALF), _mybir.dt.float32, kind="ExternalOutput").ap()
    gnn_kernel(nc, *args, out)
    got = _run(nc, [arrays], core_ids=[0]).results[0]["out_0"]
    return got.reshape(2 * BLOCKS, P, SUBS, F).transpose(0, 2, 1, 3).reshape(N, F)
```

```python
import concourse.bass as bass
from concourse import mybir
from contextlib import ExitStack

P = 128
N = 4096
F = 128
CHUNKS = N // P
BLOCKS = 4
W = N // BLOCKS
HALF = 512
SUBS = HALF // P
PAIRS = CHUNKS // 2
RING = 4
SIG_RING = 2
HI_RING = 4
LO_RING = 2
LAG = 3
GROUP = 8
LO_BY_POOL = [1, 3, 4, 6, 7]
LO_BY_DVE = []
SPLIT_IN_GROUP = sorted(LO_BY_POOL + LO_BY_DVE)
HI_BY_DVE = [1, 4, 6]
NATIVE_IN_GROUP = [k for k in range(GROUP) if k not in SPLIT_IN_GROUP]
NS, NN = len(SPLIT_IN_GROUP), len(NATIVE_IN_GROUP)
SPLIT0 = [c for c in range(CHUNKS) if c % GROUP in SPLIT_IN_GROUP]
NATIVE0 = [c for c in range(CHUNKS) if c % GROUP in NATIVE_IN_GROUP]
NSPLIT = len(SPLIT0)
POOL0 = [c for c in SPLIT0 if c % GROUP in LO_BY_POOL]
DVE0 = [c for c in SPLIT0 if c % GROUP in LO_BY_DVE]
DVE1 = [c for c in range(CHUNKS) if c % GROUP in HI_BY_DVE]
ACT1 = [c for c in range(CHUNKS) if c not in DVE1]
LN_EPS = 1e-5

F32 = mybir.dt.float32
F32R = mybir.dt.float32r
ALU = mybir.AluOpType
ACT = mybir.ActivationFunctionType



class Slots:

    def __init__(self, start, project, residual, shift, relu, turn, turned, message, msg_copy, msg_lo,
                 msg_turn, m_hi, m_lo):
        self.start, self.project, self.residual, self.shift, self.relu = start, project, residual, shift, relu
        self.turn, self.turned, self.message, self.msg_copy, self.msg_lo = turn, turned, message, msg_copy, msg_lo
        self.msg_turn, self.m_hi, self.m_lo = msg_turn, m_hi, m_lo


IN_LAYER0 = Slots([1, 15], project=0, residual=3, shift=5, relu=5, turn=4, turned=7, message=6, msg_copy=9,
                  msg_lo=10, msg_turn=8, m_hi=11, m_lo=12)
IN_LAYER1 = Slots([1, 12], project=0, residual=1, shift=2, relu=3, turn=4, turned=5, message=6, msg_copy=7,
                  msg_lo=8, msg_turn=8, m_hi=9, m_lo=10)

FIN_START = [3, 13]
FIN_START_LAST = [0, 1]
(SL_UPDATE, SL_SUM, SL_FRELU, SL_FSTATS, SL_FSHIFT, SL_FNORM) = 1, 2, 3, 4, 6, 7
SL_Q, SL_Q_HI, SL_Q_LO = 24, 25, 26


def gnn_kernel(nc, x, adj_t, weights, rows, cols, out):
    ctx = ExitStack()
    with ctx:
        def sb(name, shape, dt=F32):
            return ctx.enter_context(nc.sbuf_tensor(name, shape, dt))

        def pb(name, shape):
            return ctx.enter_context(nc.psum_tensor(name, shape, F32))

        def sem(name):
            return ctx.enter_context(nc.semaphore(name))

        adj = sb("adj", [P, RING, 2, W])
        sig = sb("sig", [P, SIG_RING, W])
        tile_hi = sb("tile_hi", [P, HI_RING, W], F32R)
        tile_lo = sb("tile_lo", [P, LO_RING, W], F32R)
        h_f32 = sb("h_f32", [P, len(NATIVE0), F])
        HQ = max(2 * W, NSPLIT * F)
        hq_hi = sb("hq_hi", [P, HQ], F32R)
        hq_lo = sb("hq_lo", [P, HQ], F32R)
        x1 = sb("x1", [P, CHUNKS, F])
        u1 = sb("u1", [P, CHUNKS, F])
        msg_hi = sb("msg_hi", [P, CHUNKS, F], F32R)
        msg_lo = sb("msg_lo", [P, CHUNKS, F], F32R)
        msgt_hi = sb("msgt_hi", [P, N], F32R)
        msgt_lo = sb("msgt_lo", [P, N], F32R)
        deg_block = sig[:, 1, :]
        agg_sb = sb("agg_sb", [P, W])
        node_a = sb("node_a", [P, SUBS, F])
        node_b = sb("node_b", [P, HALF])
        msgt_f = sb("msgt_f", [P, HALF])
        node_c = sb("node_c", [P, HALF])
        fin_rows = [node_a[:, :, :], msgt_f[:, :].rearrange("p (a f) -> p a f", a=SUBS)]
        fin_out = [node_b[:, :], node_c[:, :]]
        w_sb = sb("w_sb", [P, 6, F])
        W0, WMSG, WU_H, WU_A, WQ_T, WK_T = (w_sb[:, k, :] for k in range(6))
        rows_sb = sb("rows_sb", [P, 4 * F + 1])
        BIAS0, B_UPD, GAMMA, BETA_LN = (rows_sb[:, k * F:(k + 1) * F] for k in range(4))
        GATE_BIAS = rows_sb[:, 4 * F:4 * F + 1]
        cols_sb = sb("cols_sb", [P, CHUNKS + 1])
        B_MSG = cols_sb[:, CHUNKS:CHUNKS + 1]
        g_hi = sb("g_hi", [P, F], F32R)
        g_lo = sb("g_lo", [P, F], F32R)
        ident = sb("ident", [P, P])
        ones = sb("ones", [P, 1])
        minus_half = sb("minus_half", [P, GROUP])
        eps = sb("eps", [P, GROUP])
        stats_sb = sb("stats_sb", [P, 2 * SUBS, 6])
        mean_var_sb = sb("mean_var_sb", [P, 2 * SUBS, 2])
        ve_sb = sb("ve_sb", [P, 3, 2 * SUBS])

        def ln_half(hb):
            rows_h = slice(hb * SUBS, (hb + 1) * SUBS)
            return (stats_sb[:, rows_h, :], mean_var_sb[:, rows_h, :], ve_sb[:, 0, rows_h], ve_sb[:, 1, rows_h],
                    ve_sb[:, 2, rows_h])

        def ln_group(g):
            room = agg_sb[:, 11 * GROUP * g:11 * GROUP * (g + 1)]
            return (room[:, 0:6 * GROUP].rearrange("p (k s) -> p k s", s=6),
                    room[:, 6 * GROUP:8 * GROUP].rearrange("p (k s) -> p k s", s=2),
                    room[:, 8 * GROUP:9 * GROUP], room[:, 9 * GROUP:10 * GROUP], room[:, 10 * GROUP:11 * GROUP])

        inv_deg = sb("inv_deg", [P, W // P])

        agg_ps = pb("agg_ps", [P, W])
        logit_ps = pb("logit_ps", [P, 2, W])
        deg_sum = logit_ps[:, :, :]
        scr = pb("scr", [P, W])
        SCR0, SCR1 = scr[:, 0:HALF], scr[:, HALF:W]

        x_landed = [sem(f"x_landed{g}") for g in range(CHUNKS // GROUP)]
        w_landed = sem("w_landed")
        rows_landed = sem("rows_landed")
        cols_landed = sem("cols_landed")
        adj_landed = [sem(f"adj_landed{r}") for r in range(RING)]
        consts_ready = sem("consts_ready")
        ident_zeroed = sem("ident_zeroed")
        ident_ready = sem("ident_ready")
        bn_done = sem("bn_done")
        stats_ready = sem("stats_ready")
        eps_added = sem("eps_added")
        rstd_ready = sem("rstd_ready")
        shift_ready = sem("shift_ready")
        h_ready = sem("h_ready")
        h_hi_ready = sem("h_hi_ready")
        h_lo_ready = sem("h_lo_ready")
        bias_added = sem("bias_added")
        g_ready = sem("g_ready")
        g_hi_ready = sem("g_hi_ready")
        g_lo_ready = sem("g_lo_ready")
        diagonal_set = sem("diagonal_set")
        deg_added = sem("deg_added")
        deg_done = sem("deg_done")
        adj_hi_ready = sem("adj_hi_ready")
        adj_lo_pool = sem("adj_lo_pool")
        adj_lo_dve = sem("adj_lo_dve")
        adj_used = sem("adj_used")
        sum_copied = sem("sum_copied")
        projected = sem("projected")
        inv_ready = sem("inv_ready")
        x1_ready = sem("x1_ready")
        h2_ready = sem("h2_ready")
        h2_turned = sem("h2_turned")
        h2t_ready = sem("h2t_ready")
        msgt_ready = sem("msgt_ready")
        msgt_copied = sem("msgt_copied")
        u1_ready = sem("u1_ready")
        msgt_split = sem("msgt_split")
        msg_turned = sem("msg_turned")
        msg_hi_ready = sem("msg_hi_ready")
        msg_split = sem("msg_split")
        q_ready = sem("q_ready")
        q_hi_ready = sem("q_hi_ready")
        q_lo_ready = sem("q_lo_ready")
        logit_ready = sem("logit_ready")
        sig_ready = sem("sig_ready")
        squared = sem("squared")
        gate_ready = sem("gate_ready")
        gate_hi_act = sem("gate_hi_act")
        gate_hi_dve = sem("gate_hi_dve")
        gate_lo_ready = sem("gate_lo_ready")
        gate_used = sem("gate_used")
        updated = sem("updated")
        summed = sem("summed")
        frelu_ready = sem("frelu_ready")
        norm_ready = sem("norm_ready")
        scaled = sem("scaled")
        out_stored = sem("out_stored")

        N_GROUPS = CHUNKS // GROUP
        HALVES = 2 * BLOCKS

        def sub(ap, e):
            return ap[:, e * P:(e + 1) * P]

        def half(ap, k):
            return ap[:, k * HALF:(k + 1) * HALF]

        def h_split(c, part):
            return part[:, SPLIT0.index(c) * F:(SPLIT0.index(c) + 1) * F]

        def half_nodes(ap, b, hb):
            return ap[:, bass.ds(b * (W // P) + hb * SUBS, SUBS), :]

        def half_cols(ap, b, hb):
            return ap[:, bass.ds(b * W + hb * HALF, HALF)]

        def pair_of(c):
            return (c // 2) % RING

        def landed(eng, layer, b, c):
            eng.wait_ge(adj_landed[pair_of(c)],
                        (b + layer * BLOCKS) * (16 * PAIRS // RING) + 16 * (c // 2 // RING + 1))

        def diagonal_ready(eng, b, c):
            landed(eng, 0, b, c)
            eng.wait_ge(diagonal_set, b * PAIRS + c // 2 + 1)

        def place_free(eng, b, s, ring, first):
            if s >= ring:
                eng.wait_ge(adj_used, b * CHUNKS + SPLIT0[s - ring] + 1)
            elif not first:
                eng.wait_ge(adj_used, (b - 1) * CHUNKS + SPLIT0[s - ring] + 1)

        def wait_adj_lo(eng, b, c):
            if c in POOL0:
                eng.wait_ge(adj_lo_pool, b * len(POOL0) + POOL0.index(c) + 1)
            else:
                eng.wait_ge(adj_lo_dve, b * len(DVE0) + DVE0.index(c) + 1)

        def wait_gate_hi(eng, b, c):
            if c in ACT1:
                eng.wait_ge(gate_hi_act, b * len(ACT1) + ACT1.index(c) + 1)
            else:
                eng.wait_ge(gate_hi_dve, b * len(DVE1) + DVE1.index(c) + 1)

        def prev(b, c, back, first):
            if first and c < back:
                return None
            return b * CHUNKS + (c - back + 1)

        block = ctx.enter_context(nc.Block())

        @block.sync
        def _(sp):
            def load(layer, b, p, first=False):
                done = b * CHUNKS + 2 * (p - RING) + 2
                if first and p < RING and layer == 1:
                    done += BLOCKS * CHUNKS
                if layer == 0 and not first:
                    done = sp.snap(done)
                if layer == 0 and (p >= RING or not first) or layer == 1 and first and p < RING:
                    sp.wait_ge(adj_used, done)
                    sp.wait_ge(deg_added, done)
                elif layer == 1:
                    sp.wait_ge(gate_lo_ready, done)
                src = adj_t[bass.ds(b, 1), p].rearrange("o p g i -> (o p) g i")
                sp.dma_start(adj[:, p % RING, :, :], src).then_inc(adj_landed[p % RING], 16)

            for p in range(PAIRS):
                for g in (2 * p, 2 * p + 1) if 2 * p < N_GROUPS else ():
                    sp.dma_start(x1[:, g * GROUP:(g + 1) * GROUP, :], x[g]).then_inc(x_landed[g], 16)
                load(0, 0, p, first=True)
            with sp.Fori(1, BLOCKS) as b:
                for p in range(PAIRS):
                    load(0, b, p)
            for p in range(PAIRS):
                load(1, 0, p, first=True)

            def store(b, hb):
                sp.wait_ge(scaled, 3 * (2 * b + hb + 1))
                dst = out[bass.ds(2 * b + hb, 1)].rearrange("o p n -> (o p) n")
                sp.dma_start(dst, fin_out[hb]).then_inc(out_stored, 16)

            with sp.Fori(1, BLOCKS) as b:
                for p in range(PAIRS):
                    load(1, b, p)
                    for hb in range(2):
                        if p == (FIN_START[hb] + SL_FNORM + 3) // 2 + RING:
                            store(b - 1, hb)
            for hb in range(2):
                store(BLOCKS - 1, hb)
            sp.wait_ge(out_stored, 16 * HALVES)

        @block.tensor
        def _(pe):
            def split_products(dst, w_hi, w_lo, m_hi, m_lo, start, stop, before_lo=None):
                for k, (wt, mv) in enumerate([(w_hi, m_hi), (w_lo, m_hi), (w_hi, m_lo)]):
                    if k == 2 and before_lo is not None:
                        before_lo()
                    for hf in range(2):
                        mm = pe.matmul(half(dst, hf), wt, mv(hf), start=start and k == 0, stop=stop and k == 2)
                return mm

            pe.wait_ge(w_landed, 16)
            pe.matmul(SCR0[:, 0:F], WQ_T, WK_T, start=True, stop=True).then_inc(g_ready, 1)

            def tile0(b, c, first):
                if first and c % GROUP == 0:
                    pe.wait_ge(h_ready, c // GROUP + 1)
                    pe.wait_ge(h_lo_ready, c // GROUP + 1)
                start, stop = c == 0, c == CHUNKS - 1
                if c in NATIVE0:
                    diagonal_ready(pe, b, c)
                    for hf in range(2):
                        if start and not first:
                            pe.wait_ge(sum_copied, 2 * (b - 1) + hf + 1)
                        mm = pe.matmul(half(agg_ps, hf), h_f32[:, NATIVE0.index(c), :],
                                       half(adj[:, pair_of(c), c % 2, :], hf), start=start, stop=stop)
                else:
                    s = SPLIT0.index(c)
                    if start and not first:
                        pe.wait_ge(sum_copied, 2 * b)
                    pe.wait_ge(adj_hi_ready, b * NSPLIT + s + 1)
                    mm = split_products(agg_ps, h_split(c, hq_hi), h_split(c, hq_lo),
                                        lambda hf: half(tile_hi[:, s % HI_RING, :], hf),
                                        lambda hf: half(tile_lo[:, s % LO_RING, :], hf), start, stop,
                                        lambda: wait_adj_lo(pe, b, c))
                mm.then_inc(adj_used, 1)

            def epilogue0(b, slot, sl):
                for hb in range(2):
                    at, r = slot - sl.start[hb], 2 * b + hb
                    if at == sl.project:
                        pe.wait_ge(sum_copied, 2 * b + 2)
                        if hb == 0:
                            pe.wait_ge(deg_done, b + 1)
                        if not (isinstance(b, int) and b == 0 and hb == 0):
                            pe.wait_ge(msg_split, r)
                            pe.wait_ge(msgt_copied, 2 * r)
                        else:
                            pe.wait_ge(g_lo_ready, 1)
                        if hb == 0:
                            for e in range(W // P):
                                pe.matmul(SCR1[:, e:e + 1], sub(deg_block, e), ones[:, 0:1], start=True, stop=True)
                        for e in range(SUBS):
                            mm = pe.matmul(sub(SCR0, e), sub(agg_sb, hb * SUBS + e), W0, start=True, stop=True)
                        mm.then_inc(projected, 1)
                    if at == sl.turn:
                        pe.wait_ge(h2_ready, r + 1)
                        for e in range(SUBS):
                            mm = pe.transpose(sub(SCR0, e), node_a[:, e, :], ident[:, :])
                        mm.then_inc(h2_turned, 1)
                    if at == sl.message:
                        pe.wait_ge(h2t_ready, r + 1)
                        pe.matmul(SCR1, WMSG, node_b[:, :], start=True, stop=True).then_inc(msgt_ready, 1)
                        for e in range(SUBS):
                            mm = pe.matmul(sub(SCR0, e), sub(node_b, e), WU_H, start=True, stop=True)
                        mm.then_inc(msgt_ready, 1)
                    if at == sl.msg_turn:
                        pe.wait_ge(u1_ready, r + 1)
                        pe.wait_ge(msgt_copied, 2 * (r + 1))
                        for e in range(SUBS):
                            mm = pe.transpose(sub(SCR0, e), sub(msgt_f, e), ident[:, :])
                        mm.then_inc(msg_turned, 1)

            def query(b_next):
                for k, (wt, mv) in enumerate([(g_hi, msgt_hi), (g_lo, msgt_hi), (g_hi, msgt_lo)]):
                    for hf in range(2):
                        mm = pe.matmul(half(scr, hf), wt[:, :], half_cols(mv, b_next, hf), start=k == 0, stop=k == 2)
                mm.then_inc(q_ready, 1)

            def logits(b, c, first):
                if c == 0:
                    pe.wait_ge(q_lo_ready, b + 1)
                if first and c in (0, 24, 28):
                    pe.wait_ge(msgt_split, HALVES if c == 28 else HALVES - 1 if c == 24 else HALVES - 2)
                free = prev(b, c, 2, first)
                if free is not None:
                    pe.wait_ge(sig_ready, free)
                par = b % 2
                split_products(logit_ps[:, c % 2, :], sub(msgt_hi, c), sub(msgt_lo, c),
                               lambda hf: half_cols(hq_hi, par, hf),
                               lambda hf: half_cols(hq_lo, par, hf), True, True).then_inc(logit_ready, 1)

            def aggregate(b, c, first):
                t = b * CHUNKS + c
                if c == 0:
                    pe.wait_ge(sum_copied, 2 * (BLOCKS + b))
                if first and c in (0, 24, 28):
                    pe.wait_ge(msg_split, HALVES if c == 28 else HALVES - 1 if c == 24 else HALVES - 2)
                wait_gate_hi(pe, b, c)
                split_products(agg_ps, msg_hi[:, c, :], msg_lo[:, c, :],
                               lambda hf: half(tile_hi[:, c % HI_RING, :], hf),
                               lambda hf: half(tile_lo[:, c % LO_RING, :], hf), c == 0, c == CHUNKS - 1,
                               lambda: pe.wait_ge(gate_lo_ready, t + 1)).then_inc(gate_used, 1)

            def epilogue1(b, slot, start=FIN_START):
                for hb in range(2):
                    at, r = slot - start[hb], 2 * b + hb
                    if at == SL_UPDATE:
                        pe.wait_ge(sum_copied, 2 * (BLOCKS + b + 1))
                        pe.wait_ge(q_lo_ready, b + 2)
                        for e in range(SUBS):
                            mm = pe.matmul(sub(half(scr, hb), e), sub(agg_sb, hb * SUBS + e), WU_A, start=True, stop=True)
                        mm.then_inc(updated, 1)

            for c in range(CHUNKS):
                tile0(0, c, True)
            pe.wait_ge(ident_ready, 1)
            with pe.Fori(1, BLOCKS) as b:
                for c in range(CHUNKS):
                    tile0(b, c, False)
                    epilogue0(b - 1, c, IN_LAYER0)
            pe.wait_ge(msg_split, HALVES - 2)
            query(0)
            for c in range(CHUNKS):
                logits(0, c, True)
                if c >= LAG:
                    aggregate(0, c - LAG, True)
                epilogue0(BLOCKS - 1, c, IN_LAYER1)
                if c == SL_Q:
                    pe.wait_ge(msg_split, HALVES)
                    query(1)
            with pe.Fori(1, BLOCKS) as b:
                for c in range(CHUNKS):
                    logits(b, c, False)
                    if c >= LAG:
                        aggregate(b, c - LAG, False)
                    else:
                        aggregate(b - 1, CHUNKS - LAG + c, False)
                    epilogue1(b - 1, c)
                    if c == SL_Q:
                        pe.wait_ge(summed, 2 * b)
                        query((b + 1) % BLOCKS)
            for c in range(CHUNKS - LAG, CHUNKS):
                aggregate(BLOCKS - 1, c, False)
            for slot in range(SL_FNORM + 2):
                epilogue1(BLOCKS - 1, slot, FIN_START_LAST)

        @block.scalar
        def _(act):
            act.dma_start(rows_sb[:, :], rows.partition_broadcast(P)).then_inc(rows_landed, 16)
            act.dma_start(cols_sb[:, :], cols).then_inc(cols_landed, 16)
            act.dma_start(w_sb[:, :, :], weights).then_inc(w_landed, 16)

            def h_group(g):
                _, _, _, rstd, shift = ln_group(g)
                act.wait_ge(shift_ready, g + 1)
                for k in range(GROUP):
                    c = g * GROUP + k
                    dst = (h_f32[:, NATIVE0.index(c), :] if c in NATIVE0
                           else u1[:, g * NS + SPLIT_IN_GROUP.index(k), :])
                    i = act.activation(dst, x1[:, c, :], ACT.Relu, bias=shift[:, k:k + 1], scale=rstd[:, k:k + 1])
                i.then_inc(h_ready, 1)
                act.wait_ge(h_ready, g + 1)
                act.activation(hq_hi[:, g * NS * F:(g + 1) * NS * F],
                               u1[:, g * NS:(g + 1) * NS, :].rearrange("p a f -> p (a f)"),
                               ACT.Copy).then_inc(h_hi_ready, 1)

            def adj_hi(b, c, first):
                s = SPLIT0.index(c)
                diagonal_ready(act, b, c)
                place_free(act, b, s, HI_RING, first)
                act.activation(tile_hi[:, s % HI_RING, :], adj[:, pair_of(c), c % 2, :],
                               ACT.Copy).then_inc(adj_hi_ready, 1)

            def copy_sums(done, count, halves=(0, 1)):
                act.wait_ge(done, count)
                for hf in halves:
                    act.activation(half(agg_sb, hf), half(agg_ps, hf), ACT.Copy).then_inc(sum_copied, 1)

            def epilogue0(b, slot, sl):
                for hb in range(2):
                    at, r = slot - sl.start[hb], 2 * b + hb
                    if at == sl.relu:
                        act.wait_ge(shift_ready, N_GROUPS + r + 1)
                        _, _, _, rstd, shift = ln_half(hb)
                        for e in range(SUBS):
                            i = act.activation(node_a[:, e, :], x1[:, bass.ds(b * (W // P) + hb * SUBS + e, 1), :],
                                               ACT.Relu, bias=shift[:, e:e + 1], scale=rstd[:, e:e + 1])
                        i.then_inc(h2_ready, 1)
                    if at == sl.turned:
                        act.wait_ge(h2_turned, r + 1)
                        act.activation(node_b[:, :], SCR0, ACT.Copy).then_inc(h2t_ready, 1)
                    if at == sl.msg_copy:
                        act.wait_ge(msgt_ready, 2 * r + 1)
                        act.activation(msgt_f[:, :], SCR1, ACT.Identity, bias=B_MSG).then_inc(msgt_copied, 1)
                        act.activation(half_cols(msgt_hi, b, hb), SCR1, ACT.Identity,
                                       bias=B_MSG).then_inc(msgt_copied, 1)
                    if at == sl.m_hi:
                        act.wait_ge(msg_turned, r + 1)
                        act.activation(half_nodes(msg_hi, b, hb),
                                       SCR0.rearrange("p (a f) -> p a f", a=SUBS), ACT.Copy).then_inc(msg_hi_ready, 1)

            def q_hi(b_next):
                act.wait_ge(q_ready, b_next + 1)
                act.activation(hq_hi[:, bass.ds((b_next % 2) * W, W)], scr[:, :], ACT.Copy).then_inc(q_hi_ready, 1)

            def square(b, c):
                landed(act, 1, b, c)
                pair = adj[:, pair_of(c), :, :]
                act.activation(pair, pair, ACT.Square).then_inc(squared, 1)

            def sigmoid(b, c, first):
                act.wait_ge(logit_ready, b * CHUNKS + c + 1)
                free = prev(b, c, SIG_RING, first)
                if free is not None:
                    act.wait_ge(gate_ready, free)
                if first and c == 1:
                    act.wait_ge(projected, HALVES - 1)
                act.activation(sig[:, c % SIG_RING, :], logit_ps[:, c % 2, :], ACT.Sigmoid,
                               bias=GATE_BIAS, scale=float(F) ** -0.5).then_inc(sig_ready, 1)

            def gate_hi(b, c, first=False):
                act.wait_ge(gate_ready, b * CHUNKS + c + 1)
                free = prev(b, c, HI_RING, first)
                if free is not None:
                    act.wait_ge(gate_used, free)
                act.activation(tile_hi[:, c % HI_RING, :], adj[:, pair_of(c), c % 2, :],
                               ACT.Copy).then_inc(gate_hi_act, 1)

            def epilogue1(b, slot, start=FIN_START):
                for hb in range(2):
                    at, r = slot - start[hb], 2 * b + hb
                    if at == SL_FRELU:
                        act.wait_ge(summed, r + 1)
                        act.activation(fin_rows[hb], fin_rows[hb], ACT.Relu).then_inc(frelu_ready, 1)
                    if at == SL_FNORM:
                        act.wait_ge(shift_ready, N_GROUPS + HALVES + r + 1)
                        _, _, _, rstd, shift = ln_half(hb)
                        for e in range(SUBS):
                            i = act.activation(sub(fin_out[hb], e), fin_rows[hb][:, e, :], ACT.Identity,
                                               bias=shift[:, e:e + 1], scale=rstd[:, e:e + 1])
                        i.then_inc(norm_ready, 1)

            h_group(0)
            for c in range(CHUNKS):
                if c in (2, 8, 16):
                    h_group(c // 8 + 1)
                if c == 5:
                    act.wait_ge(g_ready, 1)
                    act.activation(g_hi[:, :], SCR0[:, 0:F], ACT.Copy).then_inc(g_hi_ready, 1)
                if c in SPLIT0:
                    adj_hi(0, c, True)
            with act.Fori(1, BLOCKS) as b:
                for c in range(CHUNKS):
                    if c in SPLIT0:
                        adj_hi(b, c, False)
                    if c == 0:
                        copy_sums(adj_used, b * CHUNKS)
                    epilogue0(b - 1, c, IN_LAYER0)
            copy_sums(adj_used, BLOCKS * CHUNKS)
            act.wait_ge(rows_landed, 16)
            q_hi(0)
            square(0, 0)
            for c in range(CHUNKS):
                sigmoid(0, c, True)
                if c - 1 in ACT1:
                    gate_hi(0, c - 1, True)
                if c % 2 == 0 and c + 2 < CHUNKS:
                    square(0, c + 2)
                epilogue0(BLOCKS - 1, c, IN_LAYER1)
                if c == SL_Q_HI:
                    q_hi(1)
            with act.Fori(1, BLOCKS) as b:
                for c in range(CHUNKS):
                    if c == 0:
                        square(b, 0)
                    sigmoid(b, c, False)
                    if c - 1 in ACT1:
                        gate_hi(b, c - 1)
                    if c == 0 and CHUNKS - 1 in ACT1:
                        gate_hi(b - 1, CHUNKS - 1)
                    if c == LAG - 1:
                        copy_sums(gate_used, b * CHUNKS)
                    if c % 2 == 0 and c + 2 < CHUNKS:
                        square(b, c + 2)
                    epilogue1(b - 1, c)
                    if c == SL_Q_HI:
                        q_hi(b + 1)
                    if c == CHUNKS - 2:
                        act.wait_ge(out_stored, 32 * b)
            if CHUNKS - 1 in ACT1:
                gate_hi(BLOCKS - 1, CHUNKS - 1)
            copy_sums(gate_used, BLOCKS * CHUNKS)
            for slot in range(SL_FNORM + 2):
                epilogue1(BLOCKS - 1, slot, FIN_START_LAST)

        @block.vector
        def _(dve):
            dve.memset(ones[:, :], 1.0).then_inc(consts_ready, 1)
            dve.memset(minus_half[:, :], -0.5).then_inc(consts_ready, 1)
            dve.memset(eps[:, :], LN_EPS).then_inc(consts_ready, 1)

            def partial_stats(parts, ln):
                for k, part in enumerate(parts):
                    i = dve.bn_stats(ln[0][:, k, :], part)
                i.then_inc(bn_done, 1)

            def whole_stats(rows_n, ln):
                for k in range(rows_n):
                    i = dve.bn_aggr(ln[1][:, k, :], ln[0][:, k, :])
                i.then_inc(stats_ready, 1)

            def layer_stats(parts, n, ln):
                partial_stats(parts, ln)
                dve.wait_ge(bn_done, n + 1)
                whole_stats(len(parts), ln)

            def layer_shift(n, ln):
                dve.wait_ge(rstd_ready, n + 1)
                dve.scalar_tensor_tensor(out=ln[4], in0=ln[1][:, :, 0], scalar=-1.0,
                                         in1=ln[3], op0=ALU.mult, op1=ALU.mult).then_inc(shift_ready, 1)

            def x_stats(g):
                dve.wait_ge(x_landed[g], 16)
                layer_stats([x1[:, g * GROUP + k, :] for k in range(GROUP)], g, ln_group(g))

            def h_lo(g):
                dve.wait_ge(h_hi_ready, g + 1)
                cols_g = slice(g * NS * F, (g + 1) * NS * F)
                dve.tensor_tensor(hq_lo[:, cols_g], u1[:, g * NS:(g + 1) * NS, :].rearrange("p a f -> p (a f)"),
                                  hq_hi[:, cols_g].bitcast(F32), ALU.subtract).then_inc(h_lo_ready, 1)

            def set_diagonal(b, p):
                landed(dve, 0, b, 2 * p)
                if p // (W // P // 2) != b:
                    dve.sem_inc(diagonal_set, 1)
                    return
                for c in (2 * p, 2 * p + 1):
                    at = sub(adj[:, pair_of(c), c % 2, :], c % (W // P))
                    i = dve.scalar_tensor_tensor(out=at, in0=ident[:, :], scalar=cols_sb[:, c:c + 1], in1=at,
                                                 op0=ALU.mult, op1=ALU.add)
                i.then_inc(diagonal_set, 1)
                dve.wait_ge(diagonal_set, b * PAIRS + p + 1)

            def add_degrees(b, p):
                here = adj[:, p % RING, :, :]
                if p == 1:
                    if b:
                        dve.wait_ge(deg_done, b)
                    dve.tensor_tensor(deg_sum, adj[:, 0, :, :], here, ALU.add).then_inc(deg_added, 4)
                elif 1 < p < PAIRS - 1:
                    dve.wait_ge(deg_added, b * CHUNKS + 2 * p)
                    dve.tensor_tensor(deg_sum, deg_sum, here, ALU.add).then_inc(deg_added, 2)
                elif p == PAIRS - 1:
                    if b > 0:
                        dve.wait_ge(projected, 2 * b - 1)
                    dve.wait_ge(deg_added, (b + 1) * CHUNKS - 2)
                    dve.tensor_tensor(deg_block, deg_sum[:, 0, :], here[:, 0, :], ALU.add).then_inc(deg_added, 1)
                    dve.wait_ge(deg_added, (b + 1) * CHUNKS - 1)
                    dve.tensor_tensor(deg_block, deg_block, here[:, 1, :], ALU.add).then_inc(deg_added, 1)
                    dve.wait_ge(deg_added, (b + 1) * CHUNKS)
                    dve.tensor_tensor(deg_block, deg_sum[:, 1, :], deg_block, ALU.add).then_inc(deg_done, 1)

            def adj_lo(b, c):
                s = SPLIT0.index(c)
                dve.wait_ge(adj_hi_ready, b * NSPLIT + s + 1)
                place_free(dve, b, s, LO_RING, b == 0)
                dve.tensor_tensor(tile_lo[:, s % LO_RING, :], adj[:, pair_of(c), c % 2, :],
                                  tile_hi[:, s % HI_RING, :].bitcast(F32), ALU.subtract).then_inc(adj_lo_dve, 1)

            def epilogue0(b, slot, sl):
                for hb in range(2):
                    at, r = slot - sl.start[hb], 2 * b + hb
                    if at == sl.residual:
                        dve.wait_ge(projected, r + 1)
                        if hb == 0:
                            dve.reciprocal(inv_deg[:, :], SCR1[:, 0:W // P]).then_inc(inv_ready, 1)
                            dve.wait_ge(inv_ready, b + 1)
                            if b == 0:
                                dve.wait_ge(bias_added, N_GROUPS)
                        for e in range(SUBS):
                            c = b * (W // P) + hb * SUBS + e
                            i = dve.scalar_tensor_tensor(
                                out=x1[:, c, :], in0=sub(SCR0, e), scalar=inv_deg[:, hb * SUBS + e:hb * SUBS + e + 1],
                                in1=x1[:, c, :], op0=ALU.mult, op1=ALU.add)
                        i.then_inc(x1_ready, 1)
                        dve.wait_ge(x1_ready, r + 1)
                        layer_stats([x1[:, b * (W // P) + hb * SUBS + e, :] for e in range(SUBS)], N_GROUPS + r,
                                    ln_half(hb))
                    if at == sl.shift:
                        layer_shift(N_GROUPS + r, ln_half(hb))
                    if at == sl.msg_copy:
                        dve.wait_ge(msgt_ready, 2 * r + 2)
                        dve.tensor_tensor(half_nodes(u1, b, hb), SCR0.rearrange("p (a f) -> p a f", a=SUBS),
                                          B_UPD.unsqueeze(1).broadcast_to([P, SUBS, F]), ALU.add).then_inc(u1_ready, 1)
                    if at == sl.msg_lo:
                        dve.wait_ge(msgt_copied, 2 * (r + 1))
                        dve.tensor_tensor(half_cols(msgt_lo, b, hb), msgt_f[:, :],
                                          half_cols(msgt_hi, b, hb).bitcast(F32), ALU.subtract).then_inc(msgt_split, 1)
                    if at == sl.m_lo:
                        dve.wait_ge(msg_hi_ready, r + 1)
                        dve.tensor_tensor(half_nodes(msg_lo, b, hb), SCR0.rearrange("p (a f) -> p a f", a=SUBS),
                                          half_nodes(msg_hi, b, hb).bitcast(F32), ALU.subtract).then_inc(msg_split, 1)

            def q_lo(b_next):
                dve.wait_ge(q_hi_ready, b_next + 1)
                at = bass.ds((b_next % 2) * W, W)
                dve.tensor_tensor(hq_lo[:, at], scr[:, :], hq_hi[:, at].bitcast(F32),
                                  ALU.subtract).then_inc(q_lo_ready, 1)

            def gates(b, c):
                t = b * CHUNKS + c
                dve.wait_ge(squared, b * PAIRS + c // 2 + 1)
                dve.wait_ge(sig_ready, t + 1)
                g = adj[:, pair_of(c), c % 2, :]
                dve.tensor_tensor(g, g, sig[:, c % SIG_RING, :], ALU.mult).then_inc(gate_ready, 1)

            def stats_wait(b, slot):
                for hb in range(2):
                    if slot == FIN_START[hb] + SL_FSTATS + 1:
                        dve.wait_ge(bn_done, N_GROUPS + HALVES + 2 * b + hb + 1)

            def gate_hi(b, c, first=False):
                dve.wait_ge(gate_ready, b * CHUNKS + c + 1)
                free = prev(b, c, HI_RING, first)
                if free is not None:
                    dve.wait_ge(gate_used, free)
                dve.tensor_copy(tile_hi[:, c % HI_RING, :], adj[:, pair_of(c), c % 2, :]).then_inc(gate_hi_dve, 1)

            def gate_lo(b, c, first=False):
                wait_gate_hi(dve, b, c)
                free = prev(b, c, LO_RING, first)
                if free is not None:
                    dve.wait_ge(gate_used, free)
                dve.tensor_tensor(tile_lo[:, c % LO_RING, :], adj[:, pair_of(c), c % 2, :],
                                  tile_hi[:, c % HI_RING, :].bitcast(F32), ALU.subtract).then_inc(gate_lo_ready, 1)

            def epilogue1(b, slot, start=FIN_START):
                for hb in range(2):
                    at, r = slot - start[hb], 2 * b + hb
                    if at == SL_SUM:
                        dve.wait_ge(updated, r + 1)
                        dve.tensor_tensor(fin_rows[hb], half(scr, hb).rearrange("p (a f) -> p a f", a=SUBS),
                                          half_nodes(u1, b, hb), ALU.add).then_inc(summed, 1)
                    if at == SL_FSTATS:
                        dve.wait_ge(frelu_ready, r + 1)
                        partial_stats([fin_rows[hb][:, e, :] for e in range(SUBS)], ln_half(hb))
                        if isinstance(b, int):
                            dve.wait_ge(bn_done, N_GROUPS + HALVES + r + 1)
                            whole_stats(SUBS, ln_half(hb))
                    if at == SL_FSTATS + 1 and not isinstance(b, int):
                        whole_stats(SUBS, ln_half(hb))
                    if at == SL_FSHIFT:
                        layer_shift(N_GROUPS + HALVES + r, ln_half(hb))

            x_stats(0)
            x_stats(1)
            layer_shift(0, ln_group(0))
            dve.wait_ge(cols_landed, 16)
            dve.wait_ge(ident_ready, 1)
            x_stats(2)
            layer_shift(1, ln_group(1))
            set_diagonal(0, 0)
            x_stats(3)
            layer_shift(2, ln_group(2))
            h_lo(0)
            for b in range(BLOCKS):
                for c in range(CHUNKS):
                    if c % 2 == 0:
                        if b or c:
                            set_diagonal(b, c // 2)
                        add_degrees(b, c // 2)
                    if b == 0 and c == 2:
                        layer_shift(3, ln_group(3))
                    if b == 0 and c in (5, 11, 17):
                        h_lo(c // 6 + 1)
                    if b == 0 and c == 6:
                        dve.wait_ge(g_hi_ready, 1)
                        dve.tensor_tensor(g_lo[:, :], SCR0[:, 0:F], g_hi[:, :].bitcast(F32),
                                          ALU.subtract).then_inc(g_lo_ready, 1)
                    if c - 1 in DVE0:
                        adj_lo(b, c - 1)
                    if b:
                        epilogue0(b - 1, c, IN_LAYER0)
            q_lo(0)
            for c in range(CHUNKS):
                gates(0, c)
                if c >= 1:
                    gate_lo(0, c - 1, True)
                if c in DVE1:
                    gate_hi(0, c, True)
                epilogue0(BLOCKS - 1, c, IN_LAYER1)
                if c == SL_Q_LO:
                    q_lo(1)
            with dve.Fori(1, BLOCKS) as b:
                for c in range(CHUNKS):
                    stats_wait(b - 1, c)
                    gates(b, c)
                    if c >= 1:
                        gate_lo(b, c - 1)
                    else:
                        gate_lo(b - 1, CHUNKS - 1)
                    if c in DVE1:
                        gate_hi(b, c)
                    epilogue1(b - 1, c)
                    if c == SL_Q_LO:
                        q_lo(b + 1)
            gate_lo(BLOCKS - 1, CHUNKS - 1)
            for slot in range(SL_FNORM + 2):
                epilogue1(BLOCKS - 1, slot, FIN_START_LAST)

        @block.gpsimd
        def _(pool):
            pool.memset(ident[:, :], 0.0).then_inc(ident_zeroed, 1)
            pool.wait_ge(ident_zeroed, 1)
            pool.affine_select(out=ident[:, :], in_=ident[:, :], compare_op=ALU.not_equal, fill=1.0, base=0,
                               pattern=[[-1, P]], channel_multiplier=1).then_inc(ident_ready, 1)
            pool.wait_ge(consts_ready, 3)

            def inv_std(n, ln):
                rows_n = ln[2].shape[1]
                pool.wait_ge(stats_ready, n + 1)
                pool.tensor_tensor(ln[2], ln[1][:, :, 1], eps[:, 0:rows_n], ALU.add).then_inc(eps_added, 1)
                pool.wait_ge(eps_added, n + 1)
                pool.tensor_tensor(ln[3], ln[2], minus_half[:, 0:rows_n], ALU.pow).then_inc(rstd_ready, 1)

            def adj_lo(b, c, first):
                s = SPLIT0.index(c)
                pool.wait_ge(adj_hi_ready, b * NSPLIT + s + 1)
                place_free(pool, b, s, LO_RING, first)
                pool.tensor_tensor(tile_lo[:, s % LO_RING, :], adj[:, pair_of(c), c % 2, :],
                                   tile_hi[:, s % HI_RING, :].bitcast(F32), ALU.subtract).then_inc(adj_lo_pool, 1)

            for g in range(N_GROUPS):
                inv_std(g, ln_group(g))
            for c in range(CHUNKS):
                if c in POOL0:
                    adj_lo(0, c, True)
                if c % GROUP == GROUP - 1:
                    g = c // GROUP
                    pool.wait_ge(rows_landed, 16)
                    pool.wait_ge(h_ready, g + 1)
                    here = x1[:, g * GROUP:(g + 1) * GROUP, :]
                    pool.tensor_tensor(here, here, BIAS0.unsqueeze(1).broadcast_to([P, GROUP, F]),
                                       ALU.add).then_inc(bias_added, 1)
            with pool.Fori(1, BLOCKS) as b:
                for c in range(CHUNKS):
                    if c in POOL0:
                        adj_lo(b, c, False)
                    for hb in range(2):
                        if c == IN_LAYER0.start[hb] + IN_LAYER0.residual:
                            inv_std(N_GROUPS + 2 * (b - 1) + hb, ln_half(hb))
            for hb in range(2):
                inv_std(N_GROUPS + 2 * (BLOCKS - 1) + hb, ln_half(hb))

            def output_step(step, y, other, r):
                pool.tensor_tensor(y, y, other, [ALU.mult, ALU.add, ALU.add][step]).then_inc(scaled, 1)
                if step < 2:
                    pool.wait_ge(scaled, 3 * r + step + 1)

            with pool.Fori(0, BLOCKS) as b:
                for hb in range(2):
                    r = 2 * b + hb
                    inv_std(N_GROUPS + HALVES + r, ln_half(hb))
                    y = fin_out[hb].rearrange("p (a f) -> p a f", a=SUBS)
                    pool.wait_ge(norm_ready, r + 1)
                    output_step(0, y, GAMMA.unsqueeze(1).broadcast_to([P, SUBS, F]), r)
                    output_step(1, y, BETA_LN.unsqueeze(1).broadcast_to([P, SUBS, F]), r)
                    output_step(2, y, half_nodes(x1, b, hb), r)


def kernel(x, adj, L0_gnn_kernel, L0_gnn_bias, L0_gnn_beta, L1_gnn_W_msg, L1_gnn_b_msg, L1_gnn_W_q, L1_gnn_W_k,
           L1_gnn_gate_bias, L1_gnn_W_upd, L1_gnn_b_upd, L1_gnn_ln_gamma, L1_gnn_ln_beta):
    import numpy as _np
    import concourse.bacc as _bacc
    from concourse import mybir as _mybir
    from concourse.bass_utils import run_bass_kernel_spmd as _run

    a = _np.asarray
    groups = CHUNKS // GROUP
    arrays = {
        "in_x": a(x).reshape(groups, GROUP, P, F).transpose(0, 2, 1, 3),
        "in_adj_t": a(adj).reshape(BLOCKS, W, PAIRS, 2, P).transpose(0, 2, 4, 3, 1),
        "in_weights": _np.stack([a(L0_gnn_kernel), a(L1_gnn_W_msg), a(L1_gnn_W_upd)[:F], a(L1_gnn_W_upd)[F:],
                                 a(L1_gnn_W_q).T, a(L1_gnn_W_k).T], axis=1),
        "in_rows": _np.concatenate([a(L0_gnn_bias), a(L1_gnn_b_upd), a(L1_gnn_ln_gamma), a(L1_gnn_ln_beta),
                                    a(L1_gnn_gate_bias).reshape(1)]),
        "in_cols": _np.concatenate([a(L0_gnn_beta).reshape(CHUNKS, P).T, a(L1_gnn_b_msg).reshape(P, 1)], axis=1),
    }
    arrays = {k: _np.ascontiguousarray(v) for k, v in arrays.items()}
    nc = _bacc.Bacc("TRN2", target_bir_lowering=False, num_devices=1)
    args = [nc.dram_tensor(k, v.shape, _mybir.dt.from_np(v.dtype), kind="ExternalInput").ap()
            for k, v in arrays.items()]
    out = nc.dram_tensor("out_0", (2 * BLOCKS, P, HALF), _mybir.dt.float32, kind="ExternalOutput").ap()
    gnn_kernel(nc, *args, out)
    got = _run(nc, [arrays], core_ids=[0]).results[0]["out_0"]
    return got.reshape(2 * BLOCKS, P, SUBS, F).transpose(0, 2, 1, 3).reshape(N, F)
```

```python
import concourse.bass as bass
from concourse import mybir
from contextlib import ExitStack

P = 128
N = 4096
F = 128
CHUNKS = N // P
BLOCKS = 4
W = N // BLOCKS
HALF = 512
SUBS = HALF // P
PAIRS = CHUNKS // 2
RING = 4
SIG_RING = 2
HI_RING = 4
LO_RING = 2
LAG = 3
SPLIT_LAG = 1
GROUP = 8
SPLIT_IN_GROUP = [1, 3, 5, 7]
NS = len(SPLIT_IN_GROUP)
SPLIT0 = [c for c in range(CHUNKS) if c % GROUP in SPLIT_IN_GROUP]
NATIVE0 = [c for c in range(CHUNKS) if c not in SPLIT0]
NSPLIT = len(SPLIT0)
SUMS_AT = 2
BIAS_AT = [20, 22, 26, 28]
DVE1 = [1, 3, 6, 11, 14, 17, 21, 23, 27, 30]
ACT1 = [c for c in range(CHUNKS) if c not in DVE1]
LN_EPS = 1e-5

F32 = mybir.dt.float32
F32R = mybir.dt.float32r
ALU = mybir.AluOpType
ACT = mybir.ActivationFunctionType



class Slots:

    def __init__(self, start, **steps):
        self.start = start
        (self.project, self.residual, self.rstd, self.shift, self.relu, self.turn, self.turned, self.message,
         self.msg_copy, self.u1, self.msg_lo, self.msg_turn, self.m_hi, self.m_lo) = (steps[k] for k in STEPS)


STEPS = ["project", "residual", "rstd", "shift", "relu", "turn", "turned", "message", "msg_copy", "u1", "msg_lo",
         "msg_turn", "m_hi", "m_lo"]
IN_LAYER0 = Slots([1, 15], project=0, residual=4, rstd=2, shift=6, relu=5, turn=5, turned=8, message=7, msg_copy=10,
                  u1=12, msg_lo=13, msg_turn=9, m_hi=12, m_lo=15)
IN_LAYER1 = Slots([0, 12], project=0, residual=1, rstd=1, shift=2, relu=3, turn=5, turned=5, message=7, msg_copy=7,
                  u1=7, msg_lo=8, msg_turn=9, m_hi=9, m_lo=10)

FIN_START = [3, 13]
FIN_START_LAST = [0, 0]
(SL_UPDATE, SL_SUM, SL_FRELU, SL_FSTATS, SL_SCALE, SL_OUT) = 1, 2, 4, 5, 7, 8
SL_Q, SL_Q_HI, SL_Q_LO = 24, 25, 26


def gnn_kernel(nc, x, adj_t, weights, rows, cols, out):
    ctx = ExitStack()
    with ctx:
        def sb(name, shape, dt=F32):
            return ctx.enter_context(nc.sbuf_tensor(name, shape, dt))

        def pb(name, shape):
            return ctx.enter_context(nc.psum_tensor(name, shape, F32))

        def sem(name):
            return ctx.enter_context(nc.semaphore(name))

        adj = sb("adj", [P, RING, 2, W])
        sig = sb("sig", [P, SIG_RING, W])
        tile_hi = sb("tile_hi", [P, HI_RING, W], F32R)
        tile_lo = sb("tile_lo", [P, LO_RING, W], F32R)
        h_more = sb("h_more", [P, len(NATIVE0) - GROUP, F])
        HQ = max(2 * W, NSPLIT * F)
        hq_hi = sb("hq_hi", [P, HQ], F32R)
        hq_lo = sb("hq_lo", [P, HQ], F32R)
        x1 = sb("x1", [P, CHUNKS, F])
        u1 = sb("u1", [P, CHUNKS, F])
        msg_hi = sb("msg_hi", [P, CHUNKS, F], F32R)
        msg_lo = sb("msg_lo", [P, CHUNKS, F], F32R)
        msgt_hi = sb("msgt_hi", [P, N], F32R)
        msgt_lo = sb("msgt_lo", [P, N], F32R)
        deg_block = sig[:, 1, :]
        agg_sb = sb("agg_sb", [P, W])
        node_a = sb("node_a", [P, SUBS, F])
        node_b = sb("node_b", [P, HALF])
        msgt_f = sb("msgt_f", [P, HALF])
        fin_rows = [node_a[:, :, :], msgt_f[:, :].rearrange("p (a f) -> p a f", a=SUBS)]
        w_sb = sb("w_sb", [P, 6, F])
        W0, WMSG, WU_H, WU_A, WQ_T, WK_T = (w_sb[:, k, :] for k in range(6))
        rows_sb = sb("rows_sb", [P, 4 * F + 1])
        BIAS0, B_UPD, GAMMA, BETA_LN = (rows_sb[:, k * F:(k + 1) * F] for k in range(4))
        GATE_BIAS = rows_sb[:, 4 * F:4 * F + 1]
        cols_sb = sb("cols_sb", [P, CHUNKS + 1])
        B_MSG = cols_sb[:, CHUNKS:CHUNKS + 1]
        g_hi = sb("g_hi", [P, F], F32R)
        g_lo = sb("g_lo", [P, F], F32R)
        ident = sb("ident", [P, P])
        ones = sb("ones", [P, 1])
        minus_half = sb("minus_half", [P, GROUP])
        eps = sb("eps", [P, GROUP])
        stats_sb = sb("stats_sb", [P, 2 * SUBS, 6])
        mean_var_sb = sb("mean_var_sb", [P, 2 * SUBS, 2])
        ve_sb = sb("ve_sb", [P, 3, 2 * SUBS])

        def ln_half(hb):
            rows_h = slice(hb * SUBS, (hb + 1) * SUBS)
            return (stats_sb[:, rows_h, :], mean_var_sb[:, rows_h, :], ve_sb[:, 0, rows_h], ve_sb[:, 1, rows_h],
                    ve_sb[:, 2, rows_h])

        def ln_group(g):
            room = agg_sb[:, 11 * GROUP * g:11 * GROUP * (g + 1)]
            return (room[:, 0:6 * GROUP].rearrange("p (k s) -> p k s", s=6),
                    room[:, 6 * GROUP:8 * GROUP].rearrange("p (k s) -> p k s", s=2),
                    room[:, 8 * GROUP:9 * GROUP], room[:, 9 * GROUP:10 * GROUP], room[:, 10 * GROUP:11 * GROUP])

        inv_deg = sb("inv_deg", [P, W // P])

        agg_ps = pb("agg_ps", [P, W])
        logit_ps = pb("logit_ps", [P, 2, W])
        deg_sum = logit_ps[:, :, :]
        scr = pb("scr", [P, W])
        SCR0, SCR1 = scr[:, 0:HALF], scr[:, HALF:W]

        x_landed = [sem(f"x_landed{g}") for g in range(CHUNKS // GROUP)]
        w_landed = sem("w_landed")
        rows_landed = sem("rows_landed")
        cols_landed = sem("cols_landed")
        adj_landed = [sem(f"adj_landed{r}") for r in range(RING)]
        consts_ready = sem("consts_ready")
        ident_zeroed = sem("ident_zeroed")
        ident_ready = sem("ident_ready")
        bn_done = sem("bn_done")
        stats_ready = sem("stats_ready")
        eps_added = sem("eps_added")
        rstd_ready = sem("rstd_ready")
        shift_ready = sem("shift_ready")
        h_ready = sem("h_ready")
        h_hi_ready = sem("h_hi_ready")
        h_lo_ready = sem("h_lo_ready")
        bias_added = sem("bias_added")
        g_ready = sem("g_ready")
        g_hi_ready = sem("g_hi_ready")
        g_lo_ready = sem("g_lo_ready")
        diagonal_set = sem("diagonal_set")
        deg_added = sem("deg_added")
        deg_done = sem("deg_done")
        adj_hi_ready = sem("adj_hi_ready")
        adj_lo_ready = sem("adj_lo_ready")
        adj_used = sem("adj_used")
        sum_copied = sem("sum_copied")
        projected = sem("projected")
        inv_ready = sem("inv_ready")
        x1_ready = sem("x1_ready")
        h2_ready = sem("h2_ready")
        h2_turned = sem("h2_turned")
        h2t_ready = sem("h2t_ready")
        msgt_ready = sem("msgt_ready")
        msgt_copied = sem("msgt_copied")
        u1_ready = sem("u1_ready")
        msgt_split = sem("msgt_split")
        msg_turned = sem("msg_turned")
        msg_hi_ready = sem("msg_hi_ready")
        msg_split = sem("msg_split")
        q_ready = sem("q_ready")
        q_hi_ready = sem("q_hi_ready")
        q_lo_ready = sem("q_lo_ready")
        logit_ready = sem("logit_ready")
        sig_ready = sem("sig_ready")
        squared = sem("squared")
        gate_ready = sem("gate_ready")
        gate_hi_act = sem("gate_hi_act")
        gate_hi_dve = sem("gate_hi_dve")
        gate_lo_ready = sem("gate_lo_ready")
        gate_used = sem("gate_used")
        updated = sem("updated")
        summed = sem("summed")
        frelu_ready = sem("frelu_ready")
        beta_added = sem("beta_added")
        scaled = sem("scaled")
        out_ready = sem("out_ready")
        out_stored = sem("out_stored")

        N_GROUPS = CHUNKS // GROUP
        HALVES = 2 * BLOCKS

        def sub(ap, e):
            return ap[:, e * P:(e + 1) * P]

        def half(ap, k):
            return ap[:, k * HALF:(k + 1) * HALF]

        def h_native(c):
            k = NATIVE0.index(c)
            return sig[:, 0, k * F:(k + 1) * F] if k < GROUP else h_more[:, k - GROUP, :]

        def h_split(c, part):
            return part[:, SPLIT0.index(c) * F:(SPLIT0.index(c) + 1) * F]

        def half_nodes(ap, b, hb):
            return ap[:, bass.ds(b * (W // P) + hb * SUBS, SUBS), :]

        def half_cols(ap, b, hb):
            return ap[:, bass.ds(b * W + hb * HALF, HALF)]

        def pair_of(c):
            return (c // 2) % RING

        def landed(eng, layer, b, c):
            eng.wait_ge(adj_landed[pair_of(c)],
                        (b + layer * BLOCKS) * (16 * PAIRS // RING) + 16 * (c // 2 // RING + 1))

        def diagonal_ready(eng, b, c):
            landed(eng, 0, b, c)
            eng.wait_ge(diagonal_set, b * PAIRS + c // 2 + 1)

        def place_free(eng, b, s, ring, first):
            if s >= ring:
                eng.wait_ge(adj_used, b * CHUNKS + SPLIT0[s - ring] + 1)
            elif not first:
                eng.wait_ge(adj_used, (b - 1) * CHUNKS + SPLIT0[s - ring] + 1)

        def wait_gate_hi(eng, b, c):
            if c in ACT1:
                eng.wait_ge(gate_hi_act, b * len(ACT1) + ACT1.index(c) + 1)
            else:
                eng.wait_ge(gate_hi_dve, b * len(DVE1) + DVE1.index(c) + 1)

        def prev(b, c, back, first):
            if first and c < back:
                return None
            return b * CHUNKS + (c - back + 1)

        block = ctx.enter_context(nc.Block())

        @block.sync
        def _(sp):
            def load(layer, b, p, first=False):
                done = b * CHUNKS + 2 * (p - RING) + 2
                if first and p < RING and layer == 1:
                    done += BLOCKS * CHUNKS
                if layer == 0 and not first:
                    done = sp.snap(done)
                if layer == 0 and (p >= RING or not first) or layer == 1 and first and p < RING:
                    sp.wait_ge(adj_used, done)
                    sp.wait_ge(deg_added, done)
                elif layer == 1:
                    sp.wait_ge(gate_lo_ready, done)
                src = adj_t[bass.ds(b, 1), p].rearrange("o p g i -> (o p) g i")
                sp.dma_start(adj[:, p % RING, :, :], src).then_inc(adj_landed[p % RING], 16)

            for g in range(N_GROUPS):
                sp.dma_start(x1[:, g * GROUP:(g + 1) * GROUP, :], x[g]).then_inc(x_landed[g], 16)
            for p in range(PAIRS):
                load(0, 0, p, first=True)
            with sp.Fori(1, BLOCKS) as b:
                for p in range(PAIRS):
                    load(0, b, p)
            for p in range(PAIRS):
                load(1, 0, p, first=True)

            def store(b, hb):
                sp.wait_ge(out_ready, 2 * b + hb + 1)
                dst = out[bass.ds(2 * b + hb, 1)].rearrange("o p n -> (o p) n")
                sp.dma_start(dst, fin_rows[hb].rearrange("p a f -> p (a f)")).then_inc(out_stored, 16)

            with sp.Fori(1, BLOCKS) as b:
                for p in range(PAIRS):
                    load(1, b, p)
                    for hb in range(2):
                        if p == (FIN_START[hb] + SL_OUT + 2) // 2 + RING:
                            store(b - 1, hb)
            for hb in range(2):
                store(BLOCKS - 1, hb)
            sp.wait_ge(out_stored, 16 * HALVES)

        @block.tensor
        def _(pe):
            def split_products(dst, w_hi, w_lo, m_hi, m_lo, start, stop, before_lo=None):
                for k, (wt, mv) in enumerate([(w_hi, m_hi), (w_lo, m_hi), (w_hi, m_lo)]):
                    if k == 2 and before_lo is not None:
                        before_lo()
                    for hf in range(2):
                        mm = pe.matmul(half(dst, hf), wt, mv(hf), start=start and k == 0, stop=stop and k == 2)
                return mm

            pe.wait_ge(w_landed, 16)
            pe.matmul(SCR0[:, 0:F], WQ_T, WK_T, start=True, stop=True).then_inc(g_ready, 1)

            def tile0(b, c, first):
                if first and c % GROUP == 0:
                    pe.wait_ge(h_ready, c // GROUP + 1)
                if first and c % GROUP == SPLIT_IN_GROUP[0]:
                    pe.wait_ge(h_lo_ready, c // GROUP + 1)
                start, stop = c == 0, c == CHUNKS - 1
                if c in NATIVE0:
                    diagonal_ready(pe, b, c)
                    for hf in range(2):
                        if start and not first:
                            pe.wait_ge(sum_copied, 2 * (b - 1) + hf + 1)
                        mm = pe.matmul(half(agg_ps, hf), h_native(c),
                                       half(adj[:, pair_of(c), c % 2, :], hf), start=start, stop=stop)
                else:
                    s = SPLIT0.index(c)
                    if start and not first:
                        pe.wait_ge(sum_copied, 2 * b)
                    pe.wait_ge(adj_hi_ready, b * NSPLIT + s + 1)
                    mm = split_products(agg_ps, h_split(c, hq_hi), h_split(c, hq_lo),
                                        lambda hf: half(tile_hi[:, s % HI_RING, :], hf),
                                        lambda hf: half(tile_lo[:, s % LO_RING, :], hf), start, stop,
                                        lambda: pe.wait_ge(adj_lo_ready, b * NSPLIT + s + 1))
                mm.then_inc(adj_used, 1)

            def epilogue0(b, slot, sl):
                for hb in range(2):
                    at, r = slot - sl.start[hb], 2 * b + hb
                    if at == sl.project:
                        pe.wait_ge(sum_copied, 2 * b + 2)
                        if hb == 0:
                            pe.wait_ge(deg_done, b + 1)
                        if not (isinstance(b, int) and b == 0 and hb == 0):
                            pe.wait_ge(msg_split, r)
                            pe.wait_ge(msgt_copied, 2 * r)
                        else:
                            pe.wait_ge(g_lo_ready, 1)
                        if hb == 0:
                            for e in range(W // P):
                                pe.matmul(SCR1[:, e:e + 1], sub(deg_block, e), ones[:, 0:1], start=True, stop=True)
                        for e in range(SUBS):
                            mm = pe.matmul(sub(SCR0, e), sub(agg_sb, hb * SUBS + e), W0, start=True, stop=True)
                        mm.then_inc(projected, 1)
                    if at == sl.turn:
                        pe.wait_ge(h2_ready, r + 1)
                        for e in range(SUBS):
                            mm = pe.transpose(sub(SCR0, e), node_a[:, e, :], ident[:, :])
                        mm.then_inc(h2_turned, 1)
                    if at == sl.message:
                        pe.wait_ge(h2t_ready, r + 1)
                        pe.matmul(SCR1, WMSG, node_b[:, :], start=True, stop=True).then_inc(msgt_ready, 1)
                        for e in range(SUBS):
                            mm = pe.matmul(sub(SCR0, e), sub(node_b, e), WU_H, start=True, stop=True)
                        mm.then_inc(msgt_ready, 1)
                    if at == sl.msg_turn:
                        pe.wait_ge(u1_ready, r + 1)
                        pe.wait_ge(msgt_copied, 2 * (r + 1))
                        for e in range(SUBS):
                            mm = pe.transpose(sub(SCR0, e), sub(msgt_f, e), ident[:, :])
                        mm.then_inc(msg_turned, 1)

            def query(b_next):
                for k, (wt, mv) in enumerate([(g_hi, msgt_hi), (g_lo, msgt_hi), (g_hi, msgt_lo)]):
                    for hf in range(2):
                        mm = pe.matmul(half(scr, hf), wt[:, :], half_cols(mv, b_next, hf), start=k == 0, stop=k == 2)
                mm.then_inc(q_ready, 1)

            def logits(b, c, first):
                if c == 0:
                    if first:
                        pe.wait_ge(deg_done, BLOCKS)
                    pe.wait_ge(q_hi_ready, b + 1)
                if first and c in (0, 24, 28):
                    pe.wait_ge(msgt_split, HALVES if c == 28 else HALVES - 1 if c == 24 else HALVES - 2)
                free = prev(b, c, 2, first)
                if free is not None:
                    pe.wait_ge(sig_ready, free)
                par = b % 2
                split_products(logit_ps[:, c % 2, :], sub(msgt_hi, c), sub(msgt_lo, c),
                               lambda hf: half_cols(hq_hi, par, hf),
                               lambda hf: half_cols(hq_lo, par, hf), True, True,
                               (lambda: pe.wait_ge(q_lo_ready, b + 1)) if c == 0 else None).then_inc(logit_ready, 1)

            def aggregate(b, c, first):
                t = b * CHUNKS + c
                if c == 0:
                    pe.wait_ge(sum_copied, 2 * (BLOCKS + b))
                if first and c in (0, 24, 28):
                    pe.wait_ge(msg_split, HALVES if c == 28 else HALVES - 1 if c == 24 else HALVES - 2)
                wait_gate_hi(pe, b, c)
                split_products(agg_ps, msg_hi[:, c, :], msg_lo[:, c, :],
                               lambda hf: half(tile_hi[:, c % HI_RING, :], hf),
                               lambda hf: half(tile_lo[:, c % LO_RING, :], hf), c == 0, c == CHUNKS - 1,
                               lambda: pe.wait_ge(gate_lo_ready, t + 1)).then_inc(gate_used, 1)

            def epilogue1(b, slot, start=FIN_START):
                for hb in range(2):
                    at, r = slot - start[hb], 2 * b + hb
                    if at == SL_UPDATE:
                        pe.wait_ge(sum_copied, 2 * (BLOCKS + b + 1))
                        pe.wait_ge(q_lo_ready, b + 2)
                        for e in range(SUBS):
                            mm = pe.matmul(sub(half(scr, hb), e), sub(agg_sb, hb * SUBS + e), WU_A, start=True, stop=True)
                        mm.then_inc(updated, 1)

            for c in range(CHUNKS):
                tile0(0, c, True)
            pe.wait_ge(ident_ready, 1)
            with pe.Fori(1, BLOCKS) as b:
                for c in range(CHUNKS):
                    tile0(b, c, False)
                    epilogue0(b - 1, c, IN_LAYER0)
            pe.wait_ge(msg_split, HALVES - 2)
            query(0)
            for c in range(CHUNKS):
                logits(0, c, True)
                if c >= LAG:
                    aggregate(0, c - LAG, True)
                epilogue0(BLOCKS - 1, c, IN_LAYER1)
                if c == SL_Q:
                    pe.wait_ge(msg_split, HALVES)
                    query(1)
            with pe.Fori(1, BLOCKS) as b:
                for c in range(CHUNKS):
                    logits(b, c, False)
                    if c >= LAG:
                        aggregate(b, c - LAG, False)
                    else:
                        aggregate(b - 1, CHUNKS - LAG + c, False)
                    epilogue1(b - 1, c)
                    if c == SL_Q:
                        pe.wait_ge(summed, 2 * b)
                        query((b + 1) % BLOCKS)
            for c in range(CHUNKS - LAG, CHUNKS):
                aggregate(BLOCKS - 1, c, False)
            for slot in range(SL_OUT + 2):
                epilogue1(BLOCKS - 1, slot, FIN_START_LAST)

        @block.scalar
        def _(act):
            act.dma_start(rows_sb[:, :], rows.partition_broadcast(P)).then_inc(rows_landed, 16)
            act.dma_start(cols_sb[:, :], cols).then_inc(cols_landed, 16)
            act.dma_start(w_sb[:, :, :], weights).then_inc(w_landed, 16)

            def h_group(g):
                _, _, _, rstd, shift = ln_group(g)
                act.wait_ge(shift_ready, g + 1)
                for k in range(GROUP):
                    c = g * GROUP + k
                    dst = (h_native(c) if c in NATIVE0
                           else u1[:, g * NS + SPLIT_IN_GROUP.index(k), :])
                    i = act.activation(dst, x1[:, c, :], ACT.Relu, bias=shift[:, k:k + 1], scale=rstd[:, k:k + 1])
                i.then_inc(h_ready, 1)
                act.wait_ge(h_ready, g + 1)
                act.activation(hq_hi[:, g * NS * F:(g + 1) * NS * F],
                               u1[:, g * NS:(g + 1) * NS, :].rearrange("p a f -> p (a f)"),
                               ACT.Copy).then_inc(h_hi_ready, 1)

            def adj_hi(b, c, first):
                s = SPLIT0.index(c)
                diagonal_ready(act, b, c)
                place_free(act, b, s, HI_RING, first)
                act.activation(tile_hi[:, s % HI_RING, :], adj[:, pair_of(c), c % 2, :],
                               ACT.Copy).then_inc(adj_hi_ready, 1)

            def copy_sums(done, count, halves=(0, 1)):
                act.wait_ge(done, count)
                for hf in halves:
                    act.activation(half(agg_sb, hf), half(agg_ps, hf), ACT.Copy).then_inc(sum_copied, 1)

            def epilogue0(b, slot, sl):
                for hb in range(2):
                    at, r = slot - sl.start[hb], 2 * b + hb
                    if at == sl.relu:
                        act.wait_ge(shift_ready, N_GROUPS + r + 1)
                        _, _, _, rstd, shift = ln_half(hb)
                        for e in range(SUBS):
                            i = act.activation(node_a[:, e, :], x1[:, bass.ds(b * (W // P) + hb * SUBS + e, 1), :],
                                               ACT.Relu, bias=shift[:, e:e + 1], scale=rstd[:, e:e + 1])
                        i.then_inc(h2_ready, 1)
                    if at == sl.turned:
                        act.wait_ge(h2_turned, r + 1)
                        act.activation(node_b[:, :], SCR0, ACT.Copy).then_inc(h2t_ready, 1)
                    if at == sl.msg_copy:
                        act.wait_ge(msgt_ready, 2 * r + 1)
                        act.activation(msgt_f[:, :], SCR1, ACT.Identity, bias=B_MSG).then_inc(msgt_copied, 1)
                        act.activation(half_cols(msgt_hi, b, hb), SCR1, ACT.Identity,
                                       bias=B_MSG).then_inc(msgt_copied, 1)
                    if at == sl.m_hi:
                        act.wait_ge(msg_turned, r + 1)
                        act.activation(half_nodes(msg_hi, b, hb),
                                       SCR0.rearrange("p (a f) -> p a f", a=SUBS), ACT.Copy).then_inc(msg_hi_ready, 1)

            def q_hi(b_next):
                act.wait_ge(q_ready, b_next + 1)
                act.activation(hq_hi[:, bass.ds((b_next % 2) * W, W)], scr[:, :], ACT.Copy).then_inc(q_hi_ready, 1)

            def square(b, c):
                landed(act, 1, b, c)
                pair = adj[:, pair_of(c), :, :]
                act.activation(pair, pair, ACT.Square).then_inc(squared, 1)

            def sigmoid(b, c, first):
                act.wait_ge(logit_ready, b * CHUNKS + c + 1)
                free = prev(b, c, SIG_RING, first)
                if free is not None:
                    act.wait_ge(gate_ready, free)
                if first and c == 1:
                    act.wait_ge(projected, HALVES - 1)
                act.activation(sig[:, c % SIG_RING, :], logit_ps[:, c % 2, :], ACT.Sigmoid,
                               bias=GATE_BIAS, scale=float(F) ** -0.5).then_inc(sig_ready, 1)

            def gate_hi(b, c, first=False):
                act.wait_ge(gate_ready, b * CHUNKS + c + 1)
                free = prev(b, c, HI_RING, first)
                if free is not None:
                    act.wait_ge(gate_used, free)
                act.activation(tile_hi[:, c % HI_RING, :], adj[:, pair_of(c), c % 2, :],
                               ACT.Copy).then_inc(gate_hi_act, 1)

            def epilogue1(b, slot, start=FIN_START):
                for hb in range(2):
                    at, r = slot - start[hb], 2 * b + hb
                    if at == SL_FRELU:
                        act.wait_ge(summed, r + 1)
                        act.activation(fin_rows[hb], fin_rows[hb], ACT.Relu).then_inc(frelu_ready, 1)

            h_group(0)
            for c in range(CHUNKS):
                if c in (2, 8, 16):
                    h_group(c // 8 + 1)
                if c == 5:
                    act.wait_ge(g_ready, 1)
                    act.activation(g_hi[:, :], SCR0[:, 0:F], ACT.Copy).then_inc(g_hi_ready, 1)
                if c in SPLIT0:
                    adj_hi(0, c, True)
            with act.Fori(1, BLOCKS) as b:
                for c in range(CHUNKS):
                    if c in SPLIT0:
                        adj_hi(b, c, False)
                    if c == SUMS_AT:
                        copy_sums(adj_used, b * CHUNKS)
                    epilogue0(b - 1, c, IN_LAYER0)
            copy_sums(adj_used, BLOCKS * CHUNKS)
            act.wait_ge(rows_landed, 16)
            q_hi(0)
            square(0, 0)
            for c in range(CHUNKS):
                sigmoid(0, c, True)
                if c - SPLIT_LAG in ACT1:
                    gate_hi(0, c - SPLIT_LAG, True)
                if c % 2 == 0 and c + 2 < CHUNKS:
                    square(0, c + 2)
                epilogue0(BLOCKS - 1, c, IN_LAYER1)
                if c == SL_Q_HI:
                    q_hi(1)
            with act.Fori(1, BLOCKS) as b:
                for c in range(CHUNKS):
                    if c == 0:
                        square(b, 0)
                    sigmoid(b, c, False)
                    if c - SPLIT_LAG in ACT1:
                        gate_hi(b, c - SPLIT_LAG)
                    if c < SPLIT_LAG and c - SPLIT_LAG + CHUNKS in ACT1:
                        gate_hi(b - 1, c - SPLIT_LAG + CHUNKS)
                    if c == LAG - 1:
                        copy_sums(gate_used, b * CHUNKS)
                    if c % 2 == 0 and c + 2 < CHUNKS:
                        square(b, c + 2)
                    epilogue1(b - 1, c)
                    if c == SL_Q_HI:
                        q_hi(b + 1)
            for c in range(CHUNKS - SPLIT_LAG, CHUNKS):
                if c in ACT1:
                    gate_hi(BLOCKS - 1, c)
            copy_sums(gate_used, BLOCKS * CHUNKS)
            for slot in range(SL_OUT + 2):
                epilogue1(BLOCKS - 1, slot, FIN_START_LAST)

        @block.vector
        def _(dve):
            dve.memset(ones[:, :], 1.0).then_inc(consts_ready, 1)
            dve.memset(minus_half[:, :], -0.5).then_inc(consts_ready, 1)
            dve.memset(eps[:, :], LN_EPS).then_inc(consts_ready, 1)

            def partial_stats(parts, ln):
                for k, part in enumerate(parts):
                    i = dve.bn_stats(ln[0][:, k, :], part)
                i.then_inc(bn_done, 1)

            def whole_stats(rows_n, ln):
                for k in range(rows_n):
                    i = dve.bn_aggr(ln[1][:, k, :], ln[0][:, k, :])
                i.then_inc(stats_ready, 1)

            def layer_stats(parts, n, ln):
                partial_stats(parts, ln)
                dve.wait_ge(bn_done, n + 1)
                whole_stats(len(parts), ln)

            def layer_shift(n, ln):
                dve.wait_ge(rstd_ready, n + 1)
                dve.scalar_tensor_tensor(out=ln[4], in0=ln[1][:, :, 0], scalar=-1.0,
                                         in1=ln[3], op0=ALU.mult, op1=ALU.mult).then_inc(shift_ready, 1)

            def x_stats(g):
                dve.wait_ge(x_landed[g], 16)
                layer_stats([x1[:, g * GROUP + k, :] for k in range(GROUP)], g, ln_group(g))

            def h_lo(g):
                dve.wait_ge(h_hi_ready, g + 1)
                cols_g = slice(g * NS * F, (g + 1) * NS * F)
                dve.tensor_tensor(hq_lo[:, cols_g], u1[:, g * NS:(g + 1) * NS, :].rearrange("p a f -> p (a f)"),
                                  hq_hi[:, cols_g].bitcast(F32), ALU.subtract).then_inc(h_lo_ready, 1)

            def set_diagonal(b, p):
                landed(dve, 0, b, 2 * p)
                if p // (W // P // 2) != b:
                    dve.sem_inc(diagonal_set, 1)
                    return
                for c in (2 * p, 2 * p + 1):
                    at = sub(adj[:, pair_of(c), c % 2, :], c % (W // P))
                    i = dve.scalar_tensor_tensor(out=at, in0=ident[:, :], scalar=cols_sb[:, c:c + 1], in1=at,
                                                 op0=ALU.mult, op1=ALU.add)
                i.then_inc(diagonal_set, 1)
                dve.wait_ge(diagonal_set, b * PAIRS + p + 1)

            def add_degrees(b, p):
                here = adj[:, p % RING, :, :]
                if p == 1:
                    if b:
                        dve.wait_ge(deg_done, b)
                    dve.tensor_tensor(deg_sum, adj[:, 0, :, :], here, ALU.add).then_inc(deg_added, 4)
                elif 1 < p < PAIRS - 1:
                    dve.wait_ge(deg_added, b * CHUNKS + 2 * p)
                    dve.tensor_tensor(deg_sum, deg_sum, here, ALU.add).then_inc(deg_added, 2)
                elif p == PAIRS - 1:
                    if b > 0:
                        dve.wait_ge(projected, 2 * b - 1)
                    dve.wait_ge(deg_added, (b + 1) * CHUNKS - 2)
                    dve.tensor_tensor(deg_block, deg_sum[:, 0, :], here[:, 0, :], ALU.add).then_inc(deg_added, 1)
                    dve.wait_ge(deg_added, (b + 1) * CHUNKS - 1)
                    dve.tensor_tensor(deg_block, deg_block, here[:, 1, :], ALU.add).then_inc(deg_added, 1)
                    dve.wait_ge(deg_added, (b + 1) * CHUNKS)
                    dve.tensor_tensor(deg_block, deg_sum[:, 1, :], deg_block, ALU.add).then_inc(deg_done, 1)

            def epilogue0(b, slot, sl):
                for hb in range(2):
                    at, r = slot - sl.start[hb], 2 * b + hb
                    if at == sl.residual:
                        dve.wait_ge(projected, r + 1)
                        if hb == 0:
                            dve.reciprocal(inv_deg[:, :], SCR1[:, 0:W // P]).then_inc(inv_ready, 1)
                            dve.wait_ge(inv_ready, b + 1)
                            if b == 0:
                                dve.wait_ge(bias_added, N_GROUPS)
                        for e in range(SUBS):
                            c = b * (W // P) + hb * SUBS + e
                            i = dve.scalar_tensor_tensor(
                                out=x1[:, c, :], in0=sub(SCR0, e), scalar=inv_deg[:, hb * SUBS + e:hb * SUBS + e + 1],
                                in1=x1[:, c, :], op0=ALU.mult, op1=ALU.add)
                        i.then_inc(x1_ready, 1)
                        dve.wait_ge(x1_ready, r + 1)
                        layer_stats([x1[:, b * (W // P) + hb * SUBS + e, :] for e in range(SUBS)], N_GROUPS + r,
                                    ln_half(hb))
                    if at == sl.shift:
                        layer_shift(N_GROUPS + r, ln_half(hb))
                    if at == sl.u1:
                        dve.wait_ge(h2_ready, r + 1)
                        dve.tensor_tensor(half_nodes(x1, b, hb), half_nodes(x1, b, hb),
                                          BETA_LN.unsqueeze(1).broadcast_to([P, SUBS, F]), ALU.add).then_inc(beta_added, 1)
                        dve.wait_ge(msgt_ready, 2 * r + 2)
                        dve.tensor_tensor(half_nodes(u1, b, hb), SCR0.rearrange("p (a f) -> p a f", a=SUBS),
                                          B_UPD.unsqueeze(1).broadcast_to([P, SUBS, F]), ALU.add).then_inc(u1_ready, 1)
                    if at == sl.msg_lo:
                        dve.wait_ge(msgt_copied, 2 * (r + 1))
                        dve.tensor_tensor(half_cols(msgt_lo, b, hb), msgt_f[:, :],
                                          half_cols(msgt_hi, b, hb).bitcast(F32), ALU.subtract).then_inc(msgt_split, 1)
                    if at == sl.m_lo:
                        dve.wait_ge(msg_hi_ready, r + 1)
                        dve.tensor_tensor(half_nodes(msg_lo, b, hb), SCR0.rearrange("p (a f) -> p a f", a=SUBS),
                                          half_nodes(msg_hi, b, hb).bitcast(F32), ALU.subtract).then_inc(msg_split, 1)

            def add_bias(g):
                dve.wait_ge(rows_landed, 16)
                dve.wait_ge(h_ready, g + 1)
                here = x1[:, g * GROUP:(g + 1) * GROUP, :]
                dve.tensor_tensor(here, here, BIAS0.unsqueeze(1).broadcast_to([P, GROUP, F]),
                                  ALU.add).then_inc(bias_added, 1)

            def q_lo(b_next):
                dve.wait_ge(q_hi_ready, b_next + 1)
                at = bass.ds((b_next % 2) * W, W)
                dve.tensor_tensor(hq_lo[:, at], scr[:, :], hq_hi[:, at].bitcast(F32),
                                  ALU.subtract).then_inc(q_lo_ready, 1)

            def gates(b, c):
                t = b * CHUNKS + c
                dve.wait_ge(squared, b * PAIRS + c // 2 + 1)
                dve.wait_ge(sig_ready, t + 1)
                g = adj[:, pair_of(c), c % 2, :]
                dve.tensor_tensor(g, g, sig[:, c % SIG_RING, :], ALU.mult).then_inc(gate_ready, 1)

            def stats_wait(b, slot):
                for hb in range(2):
                    if slot == FIN_START[hb] + SL_FSTATS + 1:
                        dve.wait_ge(bn_done, N_GROUPS + HALVES + 2 * b + hb + 1)

            def gate_hi(b, c, first=False):
                dve.wait_ge(gate_ready, b * CHUNKS + c + 1)
                free = prev(b, c, HI_RING, first)
                if free is not None:
                    dve.wait_ge(gate_used, free)
                dve.tensor_copy(tile_hi[:, c % HI_RING, :], adj[:, pair_of(c), c % 2, :]).then_inc(gate_hi_dve, 1)

            def gate_lo(b, c, first=False):
                wait_gate_hi(dve, b, c)
                free = prev(b, c, LO_RING, first)
                if free is not None:
                    dve.wait_ge(gate_used, free)
                dve.tensor_tensor(tile_lo[:, c % LO_RING, :], adj[:, pair_of(c), c % 2, :],
                                  tile_hi[:, c % HI_RING, :].bitcast(F32), ALU.subtract).then_inc(gate_lo_ready, 1)

            def epilogue1(b, slot, start=FIN_START):
                for hb in range(2):
                    at, r = slot - start[hb], 2 * b + hb
                    if at == SL_SUM:
                        dve.wait_ge(updated, r + 1)
                        dve.tensor_tensor(fin_rows[hb], half(scr, hb).rearrange("p (a f) -> p a f", a=SUBS),
                                          half_nodes(u1, b, hb), ALU.add).then_inc(summed, 1)
                    if at == SL_FSTATS:
                        dve.wait_ge(frelu_ready, r + 1)
                        partial_stats([fin_rows[hb][:, e, :] for e in range(SUBS)], ln_half(hb))
                        if isinstance(b, int):
                            dve.wait_ge(bn_done, N_GROUPS + HALVES + r + 1)
                            whole_stats(SUBS, ln_half(hb))
                    if at == SL_FSTATS + 1 and not isinstance(b, int):
                        whole_stats(SUBS, ln_half(hb))
                    if at == SL_SCALE:
                        dve.wait_ge(stats_ready, N_GROUPS + HALVES + r + 1)
                        _, mean_var, _, _, _ = ln_half(hb)
                        for e in range(SUBS):
                            here = fin_rows[hb][:, e, :]
                            i = dve.scalar_tensor_tensor(out=here, in0=here, scalar=mean_var[:, e, 0:1], in1=GAMMA,
                                                         op0=ALU.subtract, op1=ALU.mult)
                        i.then_inc(scaled, 1)
                    if at == SL_OUT:
                        dve.wait_ge(scaled, r + 1)
                        dve.wait_ge(rstd_ready, N_GROUPS + HALVES + r + 1)
                        _, _, _, rstd, _ = ln_half(hb)
                        for e in range(SUBS):
                            here = fin_rows[hb][:, e, :]
                            x1_row = x1[:, bass.ds(b * (W // P) + hb * SUBS + e, 1), :].rearrange("p a f -> p (a f)")
                            i = dve.scalar_tensor_tensor(out=here, in0=here, scalar=rstd[:, e:e + 1], in1=x1_row,
                                                         op0=ALU.mult, op1=ALU.add)
                        i.then_inc(out_ready, 1)

            x_stats(0)
            x_stats(1)
            layer_shift(0, ln_group(0))
            dve.wait_ge(cols_landed, 16)
            dve.wait_ge(ident_ready, 1)
            x_stats(2)
            layer_shift(1, ln_group(1))
            set_diagonal(0, 0)
            h_lo(0)
            x_stats(3)
            layer_shift(2, ln_group(2))
            for b in range(BLOCKS):
                for c in range(CHUNKS):
                    if c % 2 == 0:
                        if b or c:
                            set_diagonal(b, c // 2)
                        add_degrees(b, c // 2)
                    if b == 0 and c == 2:
                        layer_shift(3, ln_group(3))
                    if b == 0 and c in (6, 12, 19):
                        h_lo(c // 6)
                    if b == 0 and c == 6:
                        dve.wait_ge(g_hi_ready, 1)
                        dve.tensor_tensor(g_lo[:, :], SCR0[:, 0:F], g_hi[:, :].bitcast(F32),
                                          ALU.subtract).then_inc(g_lo_ready, 1)
                    if b == 0 and c in BIAS_AT:
                        add_bias(BIAS_AT.index(c))
                    if b:
                        epilogue0(b - 1, c, IN_LAYER0)
            q_lo(0)
            for c in range(CHUNKS):
                gates(0, c)
                if c >= SPLIT_LAG:
                    gate_lo(0, c - SPLIT_LAG, True)
                if c in DVE1:
                    gate_hi(0, c, True)
                epilogue0(BLOCKS - 1, c, IN_LAYER1)
                if c == SL_Q_LO:
                    q_lo(1)
            dve.wait_ge(beta_added, HALVES)
            with dve.Fori(1, BLOCKS) as b:
                for c in range(CHUNKS):
                    stats_wait(b - 1, c)
                    gates(b, c)
                    if c >= SPLIT_LAG:
                        gate_lo(b, c - SPLIT_LAG)
                    else:
                        gate_lo(b - 1, c - SPLIT_LAG + CHUNKS)
                    if c in DVE1:
                        gate_hi(b, c)
                    epilogue1(b - 1, c)
                    if c == SL_Q_LO:
                        q_lo(b + 1)
                    if c == CHUNKS - 2:
                        dve.wait_ge(out_stored, 32 * b)
            for c in range(CHUNKS - SPLIT_LAG, CHUNKS):
                gate_lo(BLOCKS - 1, c)
            for slot in range(SL_OUT + 2):
                epilogue1(BLOCKS - 1, slot, FIN_START_LAST)

        @block.gpsimd
        def _(pool):
            pool.memset(ident[:, :], 0.0).then_inc(ident_zeroed, 1)
            pool.wait_ge(ident_zeroed, 1)
            pool.affine_select(out=ident[:, :], in_=ident[:, :], compare_op=ALU.not_equal, fill=1.0, base=0,
                               pattern=[[-1, P]], channel_multiplier=1).then_inc(ident_ready, 1)
            pool.wait_ge(consts_ready, 3)

            def inv_std(n, ln):
                rows_n = ln[2].shape[1]
                pool.wait_ge(stats_ready, n + 1)
                pool.tensor_tensor(ln[2], ln[1][:, :, 1], eps[:, 0:rows_n], ALU.add).then_inc(eps_added, 1)
                pool.wait_ge(eps_added, n + 1)
                pool.tensor_tensor(ln[3], ln[2], minus_half[:, 0:rows_n], ALU.pow).then_inc(rstd_ready, 1)

            def adj_lo(b, c, first):
                s = SPLIT0.index(c)
                pool.wait_ge(adj_hi_ready, b * NSPLIT + s + 1)
                place_free(pool, b, s, LO_RING, first)
                pool.tensor_tensor(tile_lo[:, s % LO_RING, :], adj[:, pair_of(c), c % 2, :],
                                   tile_hi[:, s % HI_RING, :].bitcast(F32), ALU.subtract).then_inc(adj_lo_ready, 1)

            for g in range(N_GROUPS):
                inv_std(g, ln_group(g))
            for c in range(CHUNKS):
                if c in SPLIT0:
                    adj_lo(0, c, True)
            with pool.Fori(1, BLOCKS) as b:
                for c in range(CHUNKS):
                    if c in SPLIT0:
                        adj_lo(b, c, False)
                    for hb in range(2):
                        if c == IN_LAYER0.start[hb] + IN_LAYER0.rstd:
                            inv_std(N_GROUPS + 2 * (b - 1) + hb, ln_half(hb))
            for hb in range(2):
                inv_std(N_GROUPS + 2 * (BLOCKS - 1) + hb, ln_half(hb))

            with pool.Fori(0, BLOCKS) as b:
                for hb in range(2):
                    inv_std(N_GROUPS + HALVES + 2 * b + hb, ln_half(hb))


def kernel(x, adj, L0_gnn_kernel, L0_gnn_bias, L0_gnn_beta, L1_gnn_W_msg, L1_gnn_b_msg, L1_gnn_W_q, L1_gnn_W_k,
           L1_gnn_gate_bias, L1_gnn_W_upd, L1_gnn_b_upd, L1_gnn_ln_gamma, L1_gnn_ln_beta):
    import numpy as _np
    import concourse.bacc as _bacc
    from concourse import mybir as _mybir
    from concourse.bass_utils import run_bass_kernel_spmd as _run

    a = _np.asarray
    groups = CHUNKS // GROUP
    arrays = {
        "in_x": a(x).reshape(groups, GROUP, P, F).transpose(0, 2, 1, 3),
        "in_adj_t": a(adj).reshape(BLOCKS, W, PAIRS, 2, P).transpose(0, 2, 4, 3, 1),
        "in_weights": _np.stack([a(L0_gnn_kernel), a(L1_gnn_W_msg), a(L1_gnn_W_upd)[:F], a(L1_gnn_W_upd)[F:],
                                 a(L1_gnn_W_q).T, a(L1_gnn_W_k).T], axis=1),
        "in_rows": _np.concatenate([a(L0_gnn_bias), a(L1_gnn_b_upd), a(L1_gnn_ln_gamma), a(L1_gnn_ln_beta),
                                    a(L1_gnn_gate_bias).reshape(1)]),
        "in_cols": _np.concatenate([a(L0_gnn_beta).reshape(CHUNKS, P).T, a(L1_gnn_b_msg).reshape(P, 1)], axis=1),
    }
    arrays = {k: _np.ascontiguousarray(v) for k, v in arrays.items()}
    nc = _bacc.Bacc("TRN2", target_bir_lowering=False, num_devices=1)
    args = [nc.dram_tensor(k, v.shape, _mybir.dt.from_np(v.dtype), kind="ExternalInput").ap()
            for k, v in arrays.items()]
    out = nc.dram_tensor("out_0", (2 * BLOCKS, P, HALF), _mybir.dt.float32, kind="ExternalOutput").ap()
    gnn_kernel(nc, *args, out)
    got = _run(nc, [arrays], core_ids=[0]).results[0]["out_0"]
    return got.reshape(2 * BLOCKS, P, SUBS, F).transpose(0, 2, 1, 3).reshape(N, F)
```
